# Optimizing a Trainium2 kernel written in Bass

```python
import numpy as np
import jax
import jax.numpy as jnp

def _softmax(x, axis=-1):
    return jax.nn.softmax(x, axis=axis)

def _gelu(x):
    return jax.nn.gelu(x, approximate=True)

def _silu(x):
    return jax.nn.silu(x)

def _sigmoid(x):
    return jax.nn.sigmoid(x)

def _layernorm(x, axis=-1, eps=1e-05):
    m = jnp.mean(x, axis=axis, keepdims=True)
    v = jnp.var(x, axis=axis, keepdims=True)
    return (x - m) / jnp.sqrt(v + eps)

def _scatter_add(tgt, idx, src, axis=0):
    return tgt.at[idx].add(src)

def _segment_sum(src, seg, n):
    return jax.ops.segment_sum(src, seg, n)
kernel_name = 'mk_adj_resnorm_d1_adj_r2_5a28fe'

def setup_inputs(seed: int=0):
    np.random.seed(seed)
    _w = jnp.asarray

    def _rec_inputs():
        import jax
        import jax.numpy as jnp
        _gk = jax.random.key(seed)
        x = 7.22e-05 + 1 * jax.random.normal(jax.random.fold_in(_gk, 1), (128, 128, 512), jnp.float32)
        _a = jax.random.bernoulli(jax.random.fold_in(_gk, 2), 0.125, (128, 128, 128))
        _a = jnp.logical_or(_a, jnp.swapaxes(_a, -1, -2))
        _a = jnp.logical_or(_a, jnp.eye(128, dtype=bool))
        _af = _a.astype(jnp.float32)
        _af = _af * jax.random.uniform(jax.random.fold_in(_gk, 3), (128, 128, 128), jnp.float32, 0.05, 4.42607)
        adj = _af
        return (x, adj)
    x, adj = _rec_inputs()

    def _L0_gnn_setup():
        import jax, jax.numpy as jnp
        import numpy as np
        NUM_HEADS = 16
        key = jax.random.key(seed)
        ks = jax.random.split(key, 7)
        B, N, D = (16, 256, 512)
        return {'x': jax.random.normal(ks[0], (B, N, D), dtype=jnp.float32), 'spatial_encoding': jax.random.normal(ks[1], (B, N, N), dtype=jnp.float32), 'edge_encoding': jax.random.normal(ks[2], (B, N, N), dtype=jnp.float32), 'Wq': jax.random.normal(ks[3], (D, D), dtype=jnp.float32) * D ** (-0.5), 'Wk': jax.random.normal(ks[4], (D, D), dtype=jnp.float32) * D ** (-0.5), 'Wv': jax.random.normal(ks[5], (D, D), dtype=jnp.float32) * D ** (-0.5), 'Wo': jax.random.normal(ks[6], (D, D), dtype=jnp.float32) * D ** (-0.5)}
    _L0_gnn_all = _L0_gnn_setup()
    _L0_gnn_in = {k: v for k, v in _L0_gnn_all.items() if k in ('Wq', 'Wk', 'Wv', 'Wo')}
    del _L0_gnn_all
    return {'x': x, 'adj': adj, 'L0_gnn_Wq': _L0_gnn_in['Wq'], 'L0_gnn_Wk': _L0_gnn_in['Wk'], 'L0_gnn_Wv': _L0_gnn_in['Wv'], 'L0_gnn_Wo': _L0_gnn_in['Wo']}

def reference(x, adj, L0_gnn_Wq, L0_gnn_Wk, L0_gnn_Wv, L0_gnn_Wo):
    import jax
    import jax.numpy as jnp

    def _L0_gnn_ref(x, spatial_encoding, edge_encoding, Wq, Wk, Wv, Wo):
        import jax, jax.numpy as jnp
        import numpy as np
        NUM_HEADS = 16
        B, N, D = x.shape
        H = NUM_HEADS
        hd = D // H
        scale = D ** (-0.5)

        def split_heads(t):
            return t.reshape(B, N, H, hd).transpose(0, 2, 1, 3)
        q = split_heads(x @ Wq.T)
        k = split_heads(x @ Wk.T)
        v = split_heads(x @ Wv.T)
        bias = (spatial_encoding + edge_encoding)[:, None]
        a = jnp.einsum('bhnd,bhmd->bhnm', q, k) * scale + bias
        row_nonzero = jnp.any(a != 0, axis=-1, keepdims=True)
        a = jnp.where(row_nonzero, a, -jnp.inf)
        p = jax.nn.softmax(a, axis=-1)
        p = jnp.where(jnp.isnan(p), 0.0, p)
        o = jnp.einsum('bhnm,bhmd->bhnd', p, v)
        o = o.transpose(0, 2, 1, 3).reshape(B, N, D)
        return o @ Wo.T
    x = _layernorm(x + _L0_gnn_ref(x, adj, adj, L0_gnn_Wq, L0_gnn_Wk, L0_gnn_Wv, L0_gnn_Wo), axis=-1)
    return x

_drawn_inputs = setup_inputs


def setup_inputs(seed=0):
    import zlib

    import numpy as np

    out = dict(_drawn_inputs(seed))
    spreads = {}
    factors = {}
    for name, (base, spread) in spreads.items():
        noise = np.random.default_rng([zlib.crc32(name.encode()), seed]).standard_normal(out[name].shape)
        drawn = base * np.exp(spread * noise) if base else spread * noise
        out[name] = jnp.asarray(drawn.astype(out[name].dtype))
    for name, factor in factors.items():
        out[name] = (out[name] * factor).astype(out[name].dtype)
    return out
```

```python
from contextlib import ExitStack

import concourse.bass as bass
from concourse import mybir

F32 = mybir.dt.float32
F32R = mybir.dt.float32r
ALU = mybir.AluOpType
ACT = mybir.ActivationFunctionType
AX = mybir.AxisListType

P = 128
GRAPHS = 128
NODES = 128
D = 512
HEADS = 16
HD = D // HEADS
CH = D // P
GG = 4
GROUPS = GRAPHS // GG
QUADS = 4
SPG = GG * QUADS
PAIR = 2
STEPS = PAIR * SPG
ITERS = GROUPS // PAIR
GRAPHS_IT = PAIR * GG
UNITS = 3 * CH
DRAIN = 2 * QUADS
SCALE = float(D) ** -0.5
EPS = 1e-5
BIG = 3.0e38
INF = float("inf")


class Step:

    def __init__(self, m, r):
        self.m, self.r = m, r
        self.par = (r // SPG) % PAIR
        self.i = (r // QUADS) % GG
        self.j = r % QUADS

    def quad(self, lag):
        return self._count(STEPS, self.r - lag + 1, GRAPHS * QUADS)

    def graph(self, lag):
        return self._count(GRAPHS_IT, self.r // QUADS - lag + 1, GRAPHS)

    def group(self, ahead):
        return self._count(PAIR, self.r // SPG + ahead + 1, GROUPS)

    def times(self, per, const):
        return self.m * per + const

    def _count(self, per, const, most):
        n = self.m * per + const
        if isinstance(self.m, int) and not 0 < n <= most:
            return None
        return n


def build(nc, xt_d, x_d, adj_d, wq_d, wk_d, wv_d, wo_d, out_d):
    ctx = ExitStack()
    with ctx:
        def sb(name, shape, dt=F32):
            return ctx.enter_context(nc.sbuf_tensor(name, shape, dt))

        def bank(name):
            return ctx.enter_context(nc.psum_tensor(name, [P, 512], F32))

        def sem(name):
            return ctx.enter_context(nc.semaphore(name))

        w_hi = sb("w_hi", [P, 4, CH, D], F32R)
        w_lo = sb("w_lo", [P, 4, CH, D], F32R)
        xt_raw = sb("xt_raw", [P, CH, 512])
        xt_hi = sb("xt_hi", [P, PAIR, CH, 512], F32R)
        xt_lo = sb("xt_lo", [P, PAIR, CH, 512], F32R)
        q_t = sb("q_t", [P, PAIR, CH, 512])
        k_t = sb("k_t", [P, PAIR, CH, 512])
        v_sb = sb("v_sb", [P, PAIR, GG, D])
        x_sb = sb("x_sb", [P, PAIR, GG, D])
        adj_sb = sb("adj_sb", [P, PAIR, GG, NODES])
        neg_a = sb("neg_a", [P, 2, QUADS, NODES])
        e_sb = sb("e_sb", [P, 2, QUADS, NODES])
        e_t = sb("e_t", [P, 2, QUADS, NODES])
        r_wide = sb("r_wide", [P, HEADS, HD])
        r_t = sb("r_t", [P, 512])
        o_t = sb("o_t", [P, 512])
        o_hi = sb("o_hi", [P, 512], F32R)
        o_lo = sb("o_lo", [P, 512], F32R)
        ident = sb("ident", [P, P])
        ones = sb("ones", [P, 1])
        eps = sb("eps", [P, 1])
        minus_half = sb("minus_half", [P, 1])
        one_and_half = sb("one_and_half", [P, 1])
        neg_max = sb("neg_max", [P, 2, HEADS])
        neg_min = sb("neg_min", [P, 2, HEADS])
        sums = sb("sums", [P, 2, HEADS])
        abs_max = sb("abs_max", [P, HEADS])
        nonzero = sb("nonzero", [P, HEADS])
        recip = sb("recip", [P, HEADS])
        r_inv = sb("r_inv", [P, HEADS])
        ln_stats = sb("ln_stats", [P, 6])
        mean_var = sb("mean_var", [P, 2, 2])
        ln_tmp = sb("ln_tmp", [P, 6])
        rstd = sb("rstd", [P, 2])

        ps_w = [bank("ps_w0"), bank("ps_w1")]
        ps_s = [bank("ps_s0"), bank("ps_s1")]
        ps_t = [bank("ps_t0"), bank("ps_t1")]
        ps_o = bank("ps_o")
        ps_r = bank("ps_r")

        consts = sem("consts")
        w_loaded = [sem(f"w_loaded{n}") for n in range(4)]
        w_hi_done = sem("w_hi_done")
        w_lo_done = sem("w_lo_done")
        xt_loaded = sem("xt_loaded")
        x_loaded = [sem(f"x_loaded{n}") for n in range(PAIR)]
        adj_loaded = [sem(f"adj_loaded{n}") for n in range(PAIR)]
        adj_done = sem("adj_done")
        xt_hi_done = sem("xt_hi_done")
        xt_lo_done = sem("xt_lo_done")
        unit_done = sem("unit_done")
        unit_copied = sem("unit_copied")
        scores_done = sem("scores_done")
        biased = sem("biased")
        min_done = sem("min_done")
        exp_done = sem("exp_done")
        turned = sem("turned")
        turned_copied = sem("turned_copied")
        values_done = sem("values_done")
        abs_done = sem("abs_done")
        nonzero_done = sem("nonzero_done")
        recip_done = sem("recip_done")
        r_done = sem("r_done")
        r_wide_done = sem("r_wide_done")
        r_turned = sem("r_turned")
        r_copied = sem("r_copied")
        o_done = sem("o_done")
        o_hi_done = sem("o_hi_done")
        o_lo_done = sem("o_lo_done")
        out_done = sem("out_done")
        added = sem("added")
        stats_done = sem("stats_done")
        mean_done = sem("mean_done")
        pool_step = sem("pool_step")
        rstd_done = sem("rstd_done")
        normed = sem("normed")
        stored = [sem(f"stored{n}") for n in range(PAIR)]

        def iterations(eng, step, drain=0):
            for r in range(STEPS):
                step(Step(0, r))
            with eng.Fori(1, ITERS - 1) as m:
                for r in range(STEPS):
                    step(Step(m, r))
            for r in range(STEPS + drain):
                step(Step(ITERS - 1, r))

        block = ctx.enter_context(nc.Block())

        @block.sync
        def _(sp):
            sp.dma_start(xt_raw[:, :, :], xt_d[0]).then_inc(xt_loaded, 16)
            stage = [q_t[:, 1], k_t[:, 1], v_sb[:, 1], x_sb[:, 1]]
            for n, w in enumerate((wq_d, wk_d, wv_d, wo_d)):
                sp.dma_start(stage[n], w).then_inc(w_loaded[n], 16)
            sp.dma_start(adj_sb[:, 0], adj_d[0]).then_inc(adj_loaded[0], 16)
            sp.dma_start(x_sb[:, 0], x_d[0]).then_inc(x_loaded[0], 16)
            sp.wait_ge(xt_hi_done, CH)
            sp.wait_ge(xt_lo_done, CH)
            sp.dma_start(xt_raw[:, :, :], xt_d[1]).then_inc(xt_loaded, 16)
            sp.wait_ge(w_hi_done, 4)
            sp.wait_ge(w_lo_done, 4)

            def step(s):
                r16 = s.r % SPG
                if r16 == 0:
                    if (g := s.group(2)) is not None:
                        sp.wait_ge(xt_hi_done, s.times(PAIR * CH, CH * (s.r // SPG + 2)))
                        sp.wait_ge(xt_lo_done, s.times(PAIR * CH, CH * (s.r // SPG + 2)))
                        sp.dma_start(xt_raw[:, :, :], xt_d[g - 1]).then_inc(xt_loaded, 16)
                    if (g := s.group(1)) is not None:
                        if (n := s.quad(1)) is not None:
                            sp.wait_ge(biased, n)
                        sp.dma_start(adj_sb[:, 1 - s.par], adj_d[g - 1]).then_inc(adj_loaded[1 - s.par], 16)
                if s.j == 3 and (n := s.graph(2)) is not None:
                    par, i = ((s.r // QUADS - 2) // GG) % PAIR, (s.r // QUADS - 2) % GG
                    sp.wait_ge(normed, n)
                    sp.dma_start(out_d[s.times(PAIR, (s.r // QUADS - 2) // GG), :, i, :],
                                 x_sb[:, par, i, :]).then_inc(stored[par], 16)
                if r16 == 8 and (g := s.group(1)) is not None:
                    if s.group(-1) is not None:
                        sp.wait_ge(stored[1 - s.par], s.times(16 * GG, 16 * GG * s.par))
                    sp.dma_start(x_sb[:, 1 - s.par], x_d[g - 1]).then_inc(x_loaded[1 - s.par], 16)

            iterations(sp, step, DRAIN)
            for par in range(PAIR):
                sp.wait_ge(stored[par], 16 * GRAPHS // PAIR)

        @block.gpsimd
        def _(pool):
            pool.memset(ident[:, :], 0.0).then_inc(consts, 1)
            pool.memset(ones[:, :], 1.0).then_inc(consts, 1)
            pool.memset(eps[:, :], EPS).then_inc(consts, 1)
            pool.memset(minus_half[:, :], -0.5).then_inc(consts, 1)
            pool.memset(one_and_half[:, :], 1.5).then_inc(consts, 1)
            pool.wait_ge(consts, 5)
            pool.affine_select(out=ident[:, :], in_=ident[:, :], compare_op=ALU.not_equal, fill=1.0,
                               base=0, pattern=[[-1, P]], channel_multiplier=1).then_inc(consts, 1)

            def step(s):
                if s.j == 0 and (n := s.graph(1)) is not None:
                    pool.wait_ge(r_done, n)
                    if s.graph(2) is not None:
                        pool.wait_ge(r_turned, n - 1)
                    pool.tensor_tensor(r_wide[:, :, :], r_inv[:, :].unsqueeze(2).to_broadcast([P, HEADS, HD]),
                                       ones[:, :].unsqueeze(2).to_broadcast([P, HEADS, HD]),
                                       ALU.mult).then_inc(r_wide_done, 1)
                if s.j == 2 and (n := s.graph(2)) is not None:
                    b = (s.r // QUADS) % 2
                    ve, y, vy, vyy, half, rest = (ln_tmp[:, c:c + 1] for c in range(6))

                    def own(c):
                        pool.wait_ge(pool_step, s.times(6 * GRAPHS_IT, 6 * (s.r // QUADS - 2) + c))

                    pool.wait_ge(mean_done, n)
                    pool.tensor_tensor(ve, mean_var[:, b, 1:2], eps[:, :], ALU.add).then_inc(pool_step, 1)
                    own(1)
                    pool.tensor_tensor(y, ve, minus_half[:, :], ALU.pow).then_inc(pool_step, 1)
                    own(2)
                    pool.tensor_tensor(vy, ve, y, ALU.mult).then_inc(pool_step, 1)
                    own(3)
                    pool.tensor_tensor(vyy, vy, y, ALU.mult).then_inc(pool_step, 1)
                    own(4)
                    pool.tensor_tensor(half, vyy, minus_half[:, :], ALU.mult).then_inc(pool_step, 1)
                    own(5)
                    pool.tensor_tensor(rest, half, one_and_half[:, :], ALU.add).then_inc(pool_step, 1)
                    own(6)
                    pool.tensor_tensor(rstd[:, b:b + 1], y, rest, ALU.mult).then_inc(rstd_done, 1)

            iterations(pool, step, DRAIN)

        @block.tensor
        def _(pe):
            def split_product(out, lhs_hi, lhs_lo, rhs_hi, rhs_lo):
                for c in range(CH):
                    pe.matmul(out, lhs_lo(c), rhs_hi(c), start=(c == 0), stop=False)
                    pe.matmul(out, lhs_hi(c), rhs_lo(c), start=False, stop=False)
                for c in range(CH):
                    last = pe.matmul(out, lhs_hi(c), rhs_hi(c), start=False, stop=(c == CH - 1))
                return last

            def unit(u, par, out):
                n, t = u // CH, u % CH
                cols = slice(t * P, (t + 1) * P)
                if n < 2:
                    last = split_product(out, lambda c: w_hi[:, n, c, cols], lambda c: w_lo[:, n, c, cols],
                                         lambda c: xt_hi[:, par, c, :], lambda c: xt_lo[:, par, c, :])
                else:
                    last = split_product(out, lambda c: xt_hi[:, par, c, cols], lambda c: xt_lo[:, par, c, cols],
                                         lambda c: w_hi[:, 2, c, :], lambda c: w_lo[:, 2, c, :])
                last.then_inc(unit_done, 1)

            pe.wait_ge(xt_hi_done, CH)
            pe.wait_ge(xt_lo_done, CH)
            for u in range(UNITS):
                if u % CH == 0:
                    pe.wait_ge(w_hi_done, u // CH + 1)
                    pe.wait_ge(w_lo_done, u // CH + 1)
                if u >= 2:
                    pe.wait_ge(unit_copied, u - 1)
                unit(u, 0, ps_w[u % 2][:, :])
            pe.wait_ge(consts, 6)

            def step(s):
                g = s.r // SPG
                units = s.group(1) is not None
                before = 3 * s.i + s.j
                if s.quad(0) is not None:
                    if s.r % SPG == 0:
                        pe.wait_ge(unit_copied, s.times(PAIR * UNITS, UNITS * g + 2 * CH))
                    if (n := s.quad(2)) is not None:
                        pe.wait_ge(biased, n)
                    rows = slice(HD * s.j, HD * (s.j + 1))
                    nodes = slice(s.i * NODES, (s.i + 1) * NODES)
                    for t in range(QUADS):
                        last = pe.matmul(ps_s[s.r % 2][:, t * NODES:(t + 1) * NODES], q_t[rows, s.par, t, nodes],
                                         k_t[rows, s.par, t, nodes], start=True, stop=True)
                    last.then_inc(scores_done, 1)
                if s.j < 3 and units:
                    if s.r % SPG == 0:
                        pe.wait_ge(xt_hi_done, s.times(PAIR * CH, CH * (g + 2)))
                        pe.wait_ge(xt_lo_done, s.times(PAIR * CH, CH * (g + 2)))
                    if s.j == 1:
                        if (n := s.graph(2)) is not None:
                            pe.wait_ge(added, n)
                    else:
                        pe.wait_ge(unit_copied, s.times(PAIR * UNITS, UNITS * (g + 1) + before - (s.j == 2)))
                    unit(before, 1 - s.par, ps_w[s.r % 2][:, :])
                if s.j == 3 and (n := s.graph(1)) is not None:
                    if s.group(1) is not None:
                        pe.wait_ge(unit_copied, s.times(PAIR * UNITS, UNITS * (g + 1) + before - 1))
                    elif (n2 := s.graph(2)) is not None:
                        pe.wait_ge(added, n2)
                    if not isinstance(s.m, int) or s.m == 0:
                        pe.wait_ge(w_hi_done, 4)
                        pe.wait_ge(w_lo_done, 4)
                    pe.wait_ge(o_hi_done, n)
                    pe.wait_ge(o_lo_done, n)
                    split_product(ps_w[s.r % 2][:, :],
                                  lambda c: o_hi[:, c * P:(c + 1) * P], lambda c: o_lo[:, c * P:(c + 1) * P],
                                  lambda c: w_hi[:, 3, c, :], lambda c: w_lo[:, 3, c, :]).then_inc(out_done, 1)
                if (n := s.quad(2)) is not None:
                    qi, qj = ((s.r - 2) // QUADS) % GG, (s.r - 2) % QUADS
                    par = ((s.r - 2) // SPG) % PAIR
                    if (s.r - 2) % SPG == 0:
                        pe.wait_ge(unit_copied, s.times(PAIR * UNITS, UNITS * (g + 1)))
                    if qj == 0 and (n1 := s.graph(1)) is not None:
                        pe.wait_ge(o_done, n1)
                    pe.wait_ge(turned_copied, n)
                    for t in range(QUADS):
                        h = QUADS * t + qj
                        last = pe.matmul(ps_o[HD * t:HD * (t + 1), qj * P:(qj + 1) * P],
                                         v_sb[:, par, qi, h * HD:(h + 1) * HD], e_t[:, s.r % 2, t, :],
                                         start=True, stop=True)
                    last.then_inc(values_done, 1)
                if (n := s.quad(1)) is not None:
                    if (n3 := s.quad(3)) is not None:
                        pe.wait_ge(turned_copied, n3)
                    pe.wait_ge(exp_done, n)
                    b = (s.r - 1) % 2
                    for t in range(QUADS):
                        last = pe.transpose(ps_t[b][:, t * P:(t + 1) * P], e_sb[:, b, t, :], ident[:, :])
                    last.then_inc(turned, 1)
                if s.j == 0 and (n := s.graph(1)) is not None:
                    if (n2 := s.graph(2)) is not None:
                        pe.wait_ge(r_copied, n2)
                    pe.wait_ge(r_wide_done, n)
                    for q in range(QUADS):
                        last = pe.transpose(ps_r[:, q * P:(q + 1) * P],
                                            r_wide[:, QUADS * q:QUADS * (q + 1), :].rearrange("p a b -> p (a b)"),
                                            ident[:, :])
                    last.then_inc(r_turned, 1)

            iterations(pe, step, DRAIN)

        @block.scalar
        def _(act):
            def copy(out, in_, scale=1.0):
                return act.activation(out, in_, ACT.Copy, scale=scale)

            def copy_unit(u, par, in_):
                n, t = u // CH, u % CH
                out = (q_t, k_t, v_sb)[n][:, par, t, :]
                copy(out, in_, SCALE if n == 0 else 1.0).then_inc(unit_copied, 1)

            stage = [q_t[:, 1], k_t[:, 1], v_sb[:, 1], x_sb[:, 1]]

            def weight_hi(n):
                act.wait_ge(w_loaded[n], 16)
                copy(w_hi[:, n, :, :], stage[n]).then_inc(w_hi_done, 1)

            def x_hi(par, c):
                copy(xt_hi[:, par, c, :], xt_raw[:, c, :]).then_inc(xt_hi_done, 1)

            act.wait_ge(xt_loaded, 16)
            for c in range(CH):
                x_hi(0, c)
            for n in range(4):
                weight_hi(n)
            for u in range(UNITS):
                act.wait_ge(unit_done, u + 1)
                copy_unit(u, 0, ps_w[u % 2][:, :])
            act.wait_ge(xt_loaded, 32)
            for c in range(CH):
                x_hi(1, c)
            act.wait_ge(w_lo_done, 4)

            def step(s):
                g = s.r // SPG
                if s.j > 0 and s.group(1) is not None:
                    u = 3 * s.i + s.j - 1
                    act.wait_ge(unit_done, s.times(PAIR * UNITS, UNITS * (g + 1) + u + 1))
                    copy_unit(u, 1 - s.par, ps_w[(s.r - 1) % 2][:, :])
                if (n := s.quad(2)) is not None:
                    if (n4 := s.quad(4)) is not None:
                        act.wait_ge(values_done, n4)
                    act.wait_ge(turned, n)
                    b = s.r % 2
                    copy(e_t[:, b].rearrange("p a b -> p (a b)"), ps_t[b][:, :]).then_inc(turned_copied, 1)
                if s.j == 1 and (n := s.graph(1)) is not None:
                    if (n2 := s.graph(2)) is not None:
                        act.wait_ge(o_done, n2)
                    act.wait_ge(r_turned, n)
                    copy(r_t[:, :], ps_r[:, :]).then_inc(r_copied, 1)
                if s.j == 2 and (n := s.graph(1)) is not None:
                    if (n2 := s.graph(2)) is not None:
                        act.wait_ge(out_done, n2)
                    act.wait_ge(o_done, n)
                    copy(o_hi[:, :], o_t[:, :]).then_inc(o_hi_done, 1)
                if (n := s.quad(0)) is not None:
                    if (n2 := s.quad(2)) is not None:
                        act.wait_ge(turned, n2)
                    if s.j == 0 and (n2 := s.graph(2)) is not None:
                        act.wait_ge(recip_done, n2)
                    act.wait_ge(biased, n)
                    b, gb = s.r % 2, (s.r // QUADS) % 2
                    for t in range(QUADS):
                        at = QUADS * s.j + t
                        last = act.activation(e_sb[:, b, t, :], neg_a[:, b, t, :], ACT.Exp, scale=-1.0,
                                              bias=neg_max[:, gb, at:at + 1], accum_out=sums[:, gb, at:at + 1])
                    last.then_inc(exp_done, 1)
                if s.j == 3 and s.group(2) is not None:
                    if s.i == 0:
                        act.wait_ge(xt_loaded, s.times(16 * PAIR, 16 * (g + 3)))
                        act.wait_ge(unit_done, s.times(PAIR * UNITS, UNITS * (g + 1)))
                    x_hi(s.par, s.i)

            iterations(act, step, DRAIN)

        @block.vector
        def _(dve):
            def rest(out, whole, hi):
                return dve.tensor_tensor(out, whole, hi.bitcast(F32), ALU.subtract)

            def x_lo(par, c):
                rest(xt_lo[:, par, c, :], xt_raw[:, c, :], xt_hi[:, par, c, :]).then_inc(xt_lo_done, 1)

            def double_adj(par):
                adj = adj_sb[:, par].rearrange("p a b -> p (a b)")
                dve.tensor_scalar(adj, adj, 2.0, None, ALU.mult).then_inc(adj_done, 1)

            stage = [q_t[:, 1], k_t[:, 1], v_sb[:, 1], x_sb[:, 1]]
            for c in range(CH):
                dve.wait_ge(xt_hi_done, c + 1)
                x_lo(0, c)
            for n in range(4):
                dve.wait_ge(w_hi_done, n + 1)
                rest(w_lo[:, n, :, :], stage[n], w_hi[:, n, :, :]).then_inc(w_lo_done, 1)
            dve.wait_ge(adj_loaded[0], 16)
            double_adj(0)
            for c in range(CH):
                dve.wait_ge(xt_hi_done, CH + c + 1)
                x_lo(1, c)

            def step(s):
                g = s.r // SPG
                bl = s.r // QUADS
                lg = (bl - 2) // GG
                lrow = x_sb[:, lg % PAIR, (bl - 2) % GG, :]
                lb = bl % 2
                if s.j == 2 and (n := s.graph(2)) is not None:
                    dve.wait_ge(stats_done, n)
                if s.j == 2 and (n := s.graph(1)) is not None:
                    if (n2 := s.graph(2)) is not None:
                        dve.wait_ge(o_hi_done, n2)
                        dve.wait_ge(o_lo_done, n2)
                    dve.wait_ge(values_done, s.quad(3))
                    dve.wait_ge(r_copied, n)
                    dve.scalar_tensor_tensor(out=o_t[:, :], in0=ps_o[:, :], scalar=BIG, in1=r_t[:, :],
                                             op0=ALU.min, op1=ALU.mult).then_inc(o_done, 1)
                if s.j == 2 and s.graph(2) is not None:
                    dve.bn_aggr(mean_var[:, lb, :], ln_stats[:, :]).then_inc(mean_done, 1)
                if (n := s.quad(0)) is not None:
                    if s.r % SPG == 0:
                        dve.wait_ge(adj_done, s.group(0))
                    if (n2 := s.quad(2)) is not None:
                        dve.wait_ge(exp_done, n2)
                    dve.wait_ge(scores_done, n)
                if (n := s.quad(1)) is not None:
                    dve.wait_ge(biased, n)
                    qj, gb = (s.r - 1) % QUADS, ((s.r - 1) // QUADS) % 2
                    dve.tensor_reduce(neg_min[:, gb, QUADS * qj:QUADS * (qj + 1)], neg_a[:, (s.r - 1) % 2], AX.X,
                                      ALU.max).then_inc(min_done, 1)
                if s.quad(0) is not None:
                    gb = bl % 2
                    for t in range(QUADS):
                        at = QUADS * s.j + t
                        last = dve.tensor_tensor_reduce(
                            out=neg_a[:, s.r % 2, t, :], in0=ps_s[s.r % 2][:, t * NODES:(t + 1) * NODES],
                            in1=adj_sb[:, s.par, s.i, :], scale=-1.0, scalar=INF, op0=ALU.add, op1=ALU.min,
                            accum_out=neg_max[:, gb, at:at + 1])
                    last.then_inc(biased, 1)
                if s.j == 0 and (n := s.graph(1)) is not None:
                    gb = (bl - 1) % 2
                    if (n2 := s.graph(2)) is not None:
                        dve.wait_ge(r_done, n2)
                    dve.wait_ge(min_done, s.quad(1))
                    dve.scalar_tensor_tensor(out=abs_max[:, :], in0=neg_max[:, gb, :], scalar=-1.0,
                                             in1=neg_min[:, gb, :], op0=ALU.mult, op1=ALU.max).then_inc(abs_done, 1)
                    dve.wait_ge(exp_done, s.quad(1))
                    dve.reciprocal(recip[:, :], sums[:, gb, :]).then_inc(recip_done, 1)
                    dve.wait_ge(abs_done, n)
                    dve.tensor_scalar(nonzero[:, :], abs_max[:, :], 0.0, None, ALU.is_gt).then_inc(nonzero_done, 1)
                    dve.wait_ge(nonzero_done, n)
                    dve.wait_ge(recip_done, n)
                    if (n2 := s.graph(2)) is not None:
                        dve.wait_ge(r_wide_done, n2)
                    dve.scalar_tensor_tensor(out=r_inv[:, :], in0=recip[:, :], scalar=0.0, in1=nonzero[:, :],
                                             op0=ALU.max, op1=ALU.mult).then_inc(r_done, 1)
                if s.j == 0 and (n := s.graph(2)) is not None:
                    if (bl - 2) % GG == 0:
                        dve.wait_ge(x_loaded[lg % PAIR], s.times(16, 16 * (lg // PAIR + 1)))
                    dve.wait_ge(out_done, n)
                    dve.tensor_tensor(lrow, ps_w[1][:, :], lrow, ALU.add).then_inc(added, 1)
                if s.j == 1 and (n := s.graph(2)) is not None:
                    dve.wait_ge(added, n)
                    if (n3 := s.graph(3)) is not None:
                        dve.wait_ge(mean_done, n3)
                    dve.bn_stats(ln_stats[:, :], lrow).then_inc(stats_done, 1)
                if s.j == 2 and (n := s.graph(1)) is not None:
                    dve.wait_ge(o_hi_done, n)
                    if (n2 := s.graph(2)) is not None:
                        dve.wait_ge(out_done, n2)
                    rest(o_lo[:, :], o_t[:, :], o_hi[:, :]).then_inc(o_lo_done, 1)
                if s.j == 3 and (n := s.graph(2)) is not None:
                    dve.wait_ge(rstd_done, n)
                    dve.tensor_scalar(lrow, lrow, mean_var[:, lb, 0:1], rstd[:, lb:lb + 1], ALU.subtract,
                                      ALU.mult).then_inc(normed, 1)
                if s.j == 3 and s.group(2) is not None:
                    dve.wait_ge(xt_hi_done, s.times(PAIR * CH, CH * (g + 2) + s.i + 1))
                    x_lo(s.par, s.i)
                if s.r % SPG == 12 and s.group(1) is not None:
                    dve.wait_ge(adj_loaded[1 - s.par], s.times(16, 16 * (s.par + 1)))
                    double_adj(1 - s.par)

            iterations(dve, step, DRAIN)


def kernel(x, adj, L0_gnn_Wq, L0_gnn_Wk, L0_gnn_Wv, L0_gnn_Wo):
    import numpy as np
    import concourse.bacc as bacc
    from concourse.bass_utils import run_bass_kernel_spmd

    x, adj = np.asarray(x), np.asarray(adj)
    wq, wk, wv, wo = (np.asarray(w) for w in (L0_gnn_Wq, L0_gnn_Wk, L0_gnn_Wv, L0_gnn_Wo))

    def turned(w):
        return np.ascontiguousarray(w.T.reshape(CH, P, D).transpose(1, 0, 2))

    xg = x.reshape(GROUPS, GG, NODES, D)
    arrays = {
        "xt": np.ascontiguousarray(xg.reshape(GROUPS, GG * NODES, CH, P).transpose(0, 3, 2, 1)),
        "x": np.ascontiguousarray(xg.transpose(0, 2, 1, 3)),
        "adj": np.ascontiguousarray(adj.reshape(GROUPS, GG, NODES, NODES).transpose(0, 2, 1, 3)),
        "wq": turned(wq),
        "wk": turned(wk),
        "wv": turned(wv),
        "wo": np.ascontiguousarray(wo.T.reshape(QUADS, QUADS, HD, D).transpose(0, 2, 1, 3).reshape(P, QUADS, D)),
    }
    nc = bacc.Bacc("TRN2", target_bir_lowering=False, num_devices=1)
    aps = [nc.dram_tensor(name, a.shape, F32, kind="ExternalInput").ap() for name, a in arrays.items()]
    out = nc.dram_tensor("out", [GROUPS, NODES, GG, D], F32, kind="ExternalOutput").ap()
    build(nc, *aps, out)
    r = run_bass_kernel_spmd(nc, [arrays], core_ids=[0])
    got = r.results[0]["out"]
    return np.ascontiguousarray(got.transpose(0, 2, 1, 3)).reshape(GRAPHS, NODES, D)
```

```python
from contextlib import ExitStack

import concourse.bass as bass
from concourse import mybir

F32 = mybir.dt.float32
F32R = mybir.dt.float32r
ALU = mybir.AluOpType
ACT = mybir.ActivationFunctionType
AX = mybir.AxisListType

P = 128
GRAPHS = 128
NODES = 128
D = 512
HEADS = 16
HD = D // HEADS
CH = D // P
TILES = CH
TH = HEADS // TILES
GG = 4
GROUPS = GRAPHS // GG
SPG = TILES * GG
PAIR = 2
STEPS = PAIR * SPG
ITERS = GROUPS // PAIR
SCALE = float(D) ** -0.5
EPS = 1e-5
BIG = 3.0e38
INF = float("inf")

PLAN = [("q", 1, 0), ("v", 0, 1), ("v", 1, 1), ("k", 2, 0),
        ("q", 2, 0), ("o", 0, -1), ("o", 1, -1), ("k", 3, 0),
        ("q", 3, 0), ("o", 2, -1), ("o", 3, -1), ("k", 0, 1),
        ("q", 0, 1), ("v", 2, 1), ("v", 3, 1), ("k", 1, 1)]
FIRST = [("k", 0), ("q", 0), ("v", 0), ("v", 1), ("v", 2), ("v", 3), ("k", 1)]
ORDER = "kqvo"
WEIGHT = {"q": 0, "k": 1, "v": 2, "o": 3}
SPLIT_AT = 11
LN_LAG = 6
DRAIN = 10 + LN_LAG + 1


class Step:

    def __init__(self, m, r):
        self.m, self.r = m, r
        self.r16 = r % SPG
        self.par = (r // SPG) % PAIR
        self.t = self.r16 // GG
        self.i = r % GG

    def times(self, per, const):
        return self.m * per + const

    def _count(self, per, const, most):
        n = self.m * per + const
        if isinstance(self.m, int) and not 0 < n <= most:
            return None
        return n

    def quad(self, lag):
        return self._count(STEPS, self.r - lag + 1, GROUPS * SPG)

    def phase(self, lag):
        return self._count(PAIR * TILES, self.r // GG - lag + 1, GROUPS * TILES)

    def group(self, ahead):
        return self._count(PAIR, self.r // SPG + ahead + 1, GROUPS)

    def product(self, lag):
        r = self.r - lag
        kind, index, ahead = PLAN[r % SPG]
        g = r // SPG + ahead
        n = self._count(PAIR * GG, GG * g + index + 1, GRAPHS)
        return None if n is None else (kind, index, g % PAIR, n)


def o_slot(tile, par):
    return tile if tile or not par else TILES


def build(nc, xt_d, x_d, adj_d, wq_d, wk_d, wv_d, wo_d, out_d):
    ctx = ExitStack()
    with ctx:
        def sb(name, shape, dt=F32):
            return ctx.enter_context(nc.sbuf_tensor(name, shape, dt))

        def bank(name):
            return ctx.enter_context(nc.psum_tensor(name, [P, 512], F32))

        def sem(name):
            return ctx.enter_context(nc.semaphore(name))

        w_hi = sb("w_hi", [P, 4, CH, D], F32R)
        w_lo = sb("w_lo", [P, 4, CH, D], F32R)
        xt_raw = sb("xt_raw", [P, 512])
        xt_hi = sb("xt_hi", [P, PAIR, CH, 512], F32R)
        xt_lo = sb("xt_lo", [P, PAIR, CH, 512], F32R)
        q_hi = sb("q_hi", [P, 2, 512], F32R)
        q_lo = sb("q_lo", [P, 2, 512], F32R)
        k_hi = sb("k_hi", [P, 512], F32R)
        k_lo = sb("k_lo", [P, 512], F32R)
        kd_hi = sb("kd_hi", [P, 2, GG, TH * NODES], F32R)
        kd_lo = sb("kd_lo", [P, 2, GG, TH * NODES], F32R)
        v_sb = sb("v_sb", [P, PAIR, GG, D])
        x_sb = sb("x_sb", [P, GG, D])
        adj_sb = sb("adj_sb", [P, PAIR, GG, NODES])
        neg_a = sb("neg_a", [P, 2, TH, NODES])
        e_sb = sb("e_sb", [P, 2, TH, NODES])
        e_t = sb("e_t", [P, 2, TH, NODES])
        r_wide = sb("r_wide", [P, GG * TH, HD])
        ro_t = sb("ro_t", [P, 512])
        o_hi = sb("o_hi", [P, TILES + 1, 512], F32R)
        o_lo = sb("o_lo", [P, TILES + 1, 512], F32R)
        ident = sb("ident", [P, P])
        constants = sb("constants", [P, 4])
        ones, eps, minus_half, one_and_half = (constants[:, c:c + 1] for c in range(4))
        neg_max = sb("neg_max", [P, 2, GG * TH])
        neg_min = sb("neg_min", [P, 2, GG * TH])
        sums = sb("sums", [P, 2, GG * TH])
        abs_max = sb("abs_max", [P, GG * TH])
        r_inv = sb("r_inv", [P, GG * TH])
        ln_stats = sb("ln_stats", [P, 6])
        mean_var = sb("mean_var", [P, GG, 2])
        ln_tmp = sb("ln_tmp", [P, 6])
        rstd = sb("rstd", [P, GG])

        ps_w = [bank("ps_w0"), bank("ps_w1")]
        ps_s = [bank("ps_s0"), bank("ps_s1")]
        ps_t = [bank("ps_t0"), bank("ps_t1")]
        ps_o = bank("ps_o")
        ps_r = bank("ps_r")

        consts = sem("consts")
        CONSTS = 6
        zeroed = sem("zeroed")
        w_loaded = {(kind, c): sem(f"w{kind}_loaded{c}") for kind in ORDER for c in range(CH)}
        w_hi_done = sem("w_hi_done")
        w_lo_done = sem("w_lo_done")
        xt_staged = {(g, c): sem(f"xt_staged{g}{c}") for g in range(PAIR) for c in range(CH)}
        xt_loaded = sem("xt_loaded")
        x_loaded = sem("x_loaded")
        adj_loaded = [sem(f"adj_loaded{n}") for n in range(PAIR)]
        adj_done = sem("adj_done")
        xt_hi_done = sem("xt_hi_done")
        xt_lo_done = sem("xt_lo_done")
        made = {kind: sem(f"{kind}_made") for kind in "qkvo"}
        v_copied = sem("v_copied")
        q_hi_done = sem("q_hi_done")
        q_lo_done = sem("q_lo_done")
        k_hi_done = sem("k_hi_done")
        k_lo_done = sem("k_lo_done")
        kd_done = sem("kd_done")
        scores_done = sem("scores_done")
        biased = sem("biased")
        min_done = sem("min_done")
        exp_done = sem("exp_done")
        turned = sem("turned")
        turned_copied = sem("turned_copied")
        values_done = sem("values_done")
        abs_done = sem("abs_done")
        nonzero_done = sem("nonzero_done")
        recip_done = sem("recip_done")
        r_done = sem("r_done")
        r_wide_done = sem("r_wide_done")
        r_turned = sem("r_turned")
        r_copied = sem("r_copied")
        o_done = sem("o_done")
        o_hi_done = sem("o_hi_done")
        o_lo_done = sem("o_lo_done")
        added = sem("added")
        stats_done = sem("stats_done")
        mean_done = sem("mean_done")
        pool_step = sem("pool_step")
        rstd_done = sem("rstd_done")
        normed = sem("normed")
        stored = sem("stored")

        def iterations(eng, step):
            for r in range(STEPS):
                step(Step(0, r))
            with eng.Fori(1, ITERS - 1) as m:
                for r in range(STEPS):
                    step(Step(m, r))
            for r in range(STEPS + DRAIN):
                step(Step(ITERS - 1, r))

        w_stage = {"k": v_sb[:, 1], "q": x_sb[:, :, :], "v": v_sb[:, 0], "o": v_sb[:, 1]}
        xt_stage = {(g, c): buffer[:, c % 2].rearrange("p a b -> p (a b)")
                    for g, c, buffer in ((0, 0, neg_a), (0, 1, neg_a), (0, 2, e_sb), (0, 3, e_sb), (1, 0, e_t), (1, 1, e_t))}
        xt_stage[1, 2] = xt_raw[:, :]
        xt_stage[1, 3] = ro_t[:, :]

        block = ctx.enter_context(nc.Block())

        @block.sync
        def _(sp):
            def stage_w(kind, c):
                sp.dma_start(w_stage[kind][:, c], {"q": wq_d, "k": wk_d, "v": wv_d, "o": wo_d}[kind][:, c]
                             ).then_inc(w_loaded[kind, c], 16)

            def stage_chunk(g, c):
                sp.dma_start(xt_stage[g, c], xt_d[g, c]).then_inc(xt_staged[g, c], 16)

            for c in range(CH):
                stage_chunk(0, c)
                stage_w("k", c)
            for c in range(CH):
                stage_w("q", c)
            for c in range(CH):
                stage_w("v", c)
            sp.dma_start(adj_sb[:, 0], adj_d[0]).then_inc(adj_loaded[0], 16)
            for c in range(CH):
                stage_chunk(1, c)
            for c in range(CH):
                if c == 0:
                    sp.wait_ge(w_hi_done, CH)
                    sp.wait_ge(w_lo_done, CH)
                stage_w("o", c)

            def step(s):
                g = s.r // SPG
                c = 0 if s.r16 == 0 else s.r16 - SPLIT_AT
                if (s.r16 == 0 or 0 < c < CH) and (n := s.group(2)) is not None:
                    before = s.times(PAIR * CH, CH * (g + 2) + c)
                    sp.wait_ge(xt_hi_done, before)
                    sp.wait_ge(xt_lo_done, before)
                    sp.dma_start(xt_raw[:, :], xt_d[n - 1, c]).then_inc(xt_loaded, 16)
                if s.r16 == 0 and (n := s.group(1)) is not None:
                    if (n1 := s.quad(1)) is not None:
                        sp.wait_ge(biased, n1)
                    sp.dma_start(adj_sb[:, 1 - s.par], adj_d[n - 1]).then_inc(adj_loaded[1 - s.par], 16)
                if (p := s.product(LN_LAG)) is not None and p[0] == "o":
                    sp.wait_ge(normed, p[3])
                    sp.dma_start(out_d[s.times(PAIR, (s.r - LN_LAG) // SPG - 1), :, p[1], :],
                                 x_sb[:, p[1], :]).then_inc(stored, 16)
                if s.r16 == 1 and (n := s.group(-1)) is not None:
                    if s.group(-2) is not None:
                        sp.wait_ge(stored, s.times(16 * GG * PAIR, 16 * GG * (g - 1)))
                    sp.dma_start(x_sb[:, :, :], x_d[n - 1]).then_inc(x_loaded, 16)

            sp.wait_ge(w_hi_done, 2 * CH)
            sp.wait_ge(w_lo_done, 2 * CH)
            iterations(sp, step)
            sp.wait_ge(stored, 16 * GRAPHS)

        @block.gpsimd
        def _(pool):
            pool.memset(ident[:, :], 0.0).then_inc(consts, 1)
            pool.memset(ones, 1.0).then_inc(consts, 1)
            pool.memset(eps, EPS).then_inc(consts, 1)
            pool.memset(minus_half, -0.5).then_inc(consts, 1)
            pool.memset(one_and_half, 1.5).then_inc(consts, 1)
            pool.memset(kd_hi[:, :, :, :].bitcast(F32), 0.0).then_inc(zeroed, 1)
            pool.wait_ge(consts, 5)
            pool.affine_select(out=ident[:, :], in_=ident[:, :], compare_op=ALU.not_equal, fill=1.0,
                               base=0, pattern=[[-1, P]], channel_multiplier=1).then_inc(consts, 1)
            def spread(slot):
                for dense, diagonal in ((k_hi, kd_hi), (k_lo, kd_lo)):
                    for h in range(TH):
                        rows = slice(HD * h, HD * (h + 1))
                        out = diagonal[rows, slot, :, h * NODES:(h + 1) * NODES]
                        block = dense[rows, :].bitcast(F32).rearrange("p (g n) -> p g n", g=GG)
                        if dense is k_hi and h == 0:
                            pool.tensor_tensor(out, block, constants[rows, 0:1].unsqueeze(2).to_broadcast([HD, GG, NODES]),
                                               ALU.mult)
                        else:
                            last = pool.tensor_scalar(out, block, 1.0, 0.0, ALU.mult, ALU.add)
                last.then_inc(kd_done, 1)

            pool.wait_ge(zeroed, 2)
            pool.wait_ge(consts, CONSTS)
            pool.wait_ge(k_hi_done, 1)
            pool.wait_ge(k_lo_done, 1)
            spread(0)

            def latest(s, kind, lag):
                for more in range(lag, lag + 2 * SPG):
                    if (p := s.product(more)) is not None and p[0] == kind:
                        return p[3]

            def step(s):
                if s.i == 0 and (n := s.phase(1)) is not None:
                    pool.wait_ge(kd_done, latest(s, "k", 2))
                    if (n2 := s.phase(2)) is not None:
                        pool.wait_ge(r_turned, n2)
                    pool.wait_ge(r_done, n)
                    pool.tensor_tensor(r_wide[:, :, :], r_inv[:, :].unsqueeze(2).to_broadcast([P, GG * TH, HD]),
                                       ones.unsqueeze(2).to_broadcast([P, GG * TH, HD]),
                                       ALU.mult).then_inc(r_wide_done, 1)
                if (p := s.product(1)) is not None and p[0] == "k":
                    pool.wait_ge(k_hi_done, p[3])
                    pool.wait_ge(k_lo_done, p[3])
                    if (n1 := s.quad(1)) is not None:
                        pool.wait_ge(scores_done, n1)
                    if (n1 := s.phase(1)) is not None:
                        pool.wait_ge(r_wide_done, n1)
                    if (n1 := latest(s, "o", 4)) is not None:
                        pool.wait_ge(rstd_done, n1)
                    spread(p[1] % 2)
                if (p := s.product(3)) is not None and p[0] == "o":
                    i = p[1]
                    ve, y, vy, vyy, half, rest = (ln_tmp[:, c:c + 1] for c in range(6))
                    before = GG * ((s.r - 3) // SPG - 1) + i

                    def own(c):
                        pool.wait_ge(pool_step, s.times(6 * PAIR * GG, 6 * before + c))

                    pool.wait_ge(kd_done, latest(s, "k", 1))
                    pool.wait_ge(mean_done, p[3])
                    pool.tensor_tensor(ve, mean_var[:, i, 1:2], eps, ALU.add).then_inc(pool_step, 1)
                    own(1)
                    pool.tensor_tensor(y, ve, minus_half, ALU.pow).then_inc(pool_step, 1)
                    own(2)
                    pool.tensor_tensor(vy, ve, y, ALU.mult).then_inc(pool_step, 1)
                    own(3)
                    pool.tensor_tensor(vyy, vy, y, ALU.mult).then_inc(pool_step, 1)
                    own(4)
                    pool.tensor_tensor(half, vyy, minus_half, ALU.mult).then_inc(pool_step, 1)
                    own(5)
                    pool.tensor_tensor(rest, half, one_and_half, ALU.add).then_inc(pool_step, 1)
                    own(6)
                    pool.tensor_tensor(rstd[:, i:i + 1], y, rest, ALU.mult).then_inc(rstd_done, 1)

            iterations(pool, step)

        @block.tensor
        def _(pe):
            def split_product(out, chunks, lhs_hi, lhs_lo, rhs_hi, rhs_lo, before=None):
                for c in range(chunks):
                    if before:
                        before(c)
                    pe.matmul(out, lhs_lo(c), rhs_hi(c), start=(c == 0), stop=False)
                    pe.matmul(out, lhs_hi(c), rhs_lo(c), start=False, stop=False)
                for c in range(chunks):
                    last = pe.matmul(out, lhs_hi(c), rhs_hi(c), start=False, stop=(c == chunks - 1))
                return last

            def weight_product(kind, index, par, out, before=None):
                w, cols = WEIGHT[kind], slice(index * P, (index + 1) * P)
                if kind in "qk":
                    last = split_product(out, CH, lambda c: w_hi[:, w, c, cols], lambda c: w_lo[:, w, c, cols],
                                         lambda c: xt_hi[:, par, c, :], lambda c: xt_lo[:, par, c, :], before)
                elif kind == "v":
                    last = split_product(out, CH, lambda c: xt_hi[:, par, c, cols], lambda c: xt_lo[:, par, c, cols],
                                         lambda c: w_hi[:, w, c, :], lambda c: w_lo[:, w, c, :], before)
                else:
                    last = split_product(out, CH, lambda c: o_hi[:, o_slot(c, par), cols],
                                         lambda c: o_lo[:, o_slot(c, par), cols],
                                         lambda c: w_hi[:, w, c, :], lambda c: w_lo[:, w, c, :], before)
                last.then_inc(made[kind], 1)

            released = {"v": v_copied, "k": k_lo_done, "q": q_lo_done, "o": added}

            for u, (kind, index) in enumerate(FIRST):
                def before(c):
                    n = CH * ORDER.index(kind) + c + 1
                    if kind == "k":
                        pe.wait_ge(xt_hi_done, c + 1)
                        pe.wait_ge(xt_lo_done, c + 1)
                    pe.wait_ge(w_hi_done, n)
                    pe.wait_ge(w_lo_done, n)
                if u >= 2:
                    k2, i2 = FIRST[u - 2]
                    pe.wait_ge(released[k2], i2 + 1)
                weight_product(kind, index, 0, ps_w[(u + 1) % 2][:, :], before if index == 0 else None)
            pe.wait_ge(consts, CONSTS)

            def step(s):
                b = s.r % 2
                if s.quad(0) is not None:
                    if s.i == 0:
                        pe.wait_ge(kd_done, s.phase(0))
                        pe.wait_ge(q_lo_done, s.phase(0))
                    if (n := s.quad(2)) is not None:
                        pe.wait_ge(biased, n)
                    slot, nodes = s.t % 2, slice(s.i * NODES, (s.i + 1) * NODES)
                    split_product(ps_s[b][:, :], 1, lambda c: q_hi[:, slot, nodes], lambda c: q_lo[:, slot, nodes],
                                  lambda c: kd_hi[:, slot, s.i, :], lambda c: kd_lo[:, slot, s.i, :]
                                  ).then_inc(scores_done, 1)
                if (p := s.product(0)) is not None:
                    kind, index, par, n = p
                    for lag in range(2, SPG, 2):
                        if (p2 := s.product(lag)) is not None:
                            pe.wait_ge(released[p2[0]], p2[3])
                            break
                    if kind == "v" and index == 0:
                        pe.wait_ge(xt_hi_done, s.times(PAIR * CH, CH * (s.r // SPG + 2)))
                        pe.wait_ge(xt_lo_done, s.times(PAIR * CH, CH * (s.r // SPG + 2)))
                    if kind == "o" and index == 0:
                        if not isinstance(s.m, int) or s.m == 0:
                            pe.wait_ge(w_hi_done, 4 * CH)
                            pe.wait_ge(w_lo_done, 4 * CH)
                        pe.wait_ge(o_hi_done, s.times(PAIR * TILES, TILES * (s.r // SPG)))
                        pe.wait_ge(o_lo_done, s.times(PAIR * TILES, TILES * (s.r // SPG)))
                    weight_product(kind, index, par, ps_w[b][:, :])
                if s.i == 1 and (n := s.phase(1)) is not None:
                    if (n2 := s.phase(2)) is not None:
                        pe.wait_ge(r_copied, n2)
                    pe.wait_ge(r_wide_done, n)
                    for i in range(GG):
                        last = pe.transpose(ps_r[:, i * P:(i + 1) * P],
                                            r_wide[:, TH * i:TH * (i + 1), :].rearrange("p a b -> p (a b)"),
                                            ident[:, :])
                    last.then_inc(r_turned, 1)
                if (n := s.quad(2)) is not None:
                    r2 = s.r - 2
                    par, t, i = (r2 // SPG) % PAIR, (r2 % SPG) // GG, r2 % GG
                    if r2 % SPG < GG:
                        pe.wait_ge(v_copied, s.times(PAIR * GG, GG * (r2 // SPG) + i + 1))
                    if i == 0 and (n1 := s.phase(1)) is not None:
                        pe.wait_ge(o_done, n1)
                    pe.wait_ge(turned_copied, n)
                    for h in range(TH):
                        cols = slice((TH * t + h) * HD, (TH * t + h + 1) * HD)
                        last = pe.matmul(ps_o[HD * h:HD * (h + 1), i * P:(i + 1) * P], v_sb[:, par, i, cols],
                                         e_t[:, b, h, :], start=True, stop=True)
                    last.then_inc(values_done, 1)
                if (n := s.quad(1)) is not None:
                    if (n3 := s.quad(3)) is not None:
                        pe.wait_ge(turned_copied, n3)
                    pe.wait_ge(exp_done, n)
                    for h in range(TH):
                        last = pe.transpose(ps_t[1 - b][:, h * P:(h + 1) * P], e_sb[:, 1 - b, h, :], ident[:, :])
                    last.then_inc(turned, 1)

            iterations(pe, step)

        @block.scalar
        def _(act):
            def copy(out, in_, scale=1.0):
                return act.activation(out, in_, ACT.Copy, scale=scale)

            def take(kind, index, par, n, in_, later):
                act.wait_ge(made[kind], n)
                if kind == "v":
                    copy(v_sb[:, par, index, :], in_).then_inc(v_copied, 1)
                elif kind == "q":
                    copy(q_hi[:, index % 2, :], in_, SCALE).then_inc(q_hi_done, 1)
                elif kind == "k":
                    if later:
                        act.wait_ge(kd_done, n - 1)
                    copy(k_hi[:, :], in_).then_inc(k_hi_done, 1)

            def weight_hi(kind, c):
                act.wait_ge(w_loaded[kind, c], 16)
                copy(w_hi[:, WEIGHT[kind], c, :], w_stage[kind][:, c]).then_inc(w_hi_done, 1)

            def staged_hi(g, c):
                act.wait_ge(xt_staged[g, c], 16)
                copy(xt_hi[:, g, c, :], xt_stage[g, c]).then_inc(xt_hi_done, 1)

            def first(u):
                kind, index = FIRST[u]
                take(kind, index, 0, index + 1, ps_w[(u + 1) % 2][:, :], False)

            for c in range(CH):
                staged_hi(0, c)
                weight_hi("k", c)
            for c in range(CH):
                weight_hi("q", c)
            first(0)
            for c in range(CH):
                weight_hi("v", c)
            first(1)
            first(2)
            for c in range(CH):
                staged_hi(1, c)
            first(3)
            for c in range(CH):
                weight_hi("o", c)
            first(4)
            first(5)

            def step(s):
                b = s.r % 2
                if (p := s.product(1)) is not None and p[0] != "o":
                    kind, index, par, n = p
                    if isinstance(s.m, int) and s.m == 0 and (kind, par, index) == ("v", 1, 0):
                        act.wait_ge(w_lo_done, 4 * CH)
                    take(kind, index, par, n, ps_w[1 - b][:, :], True)
                if (n := s.quad(2)) is not None:
                    if (n4 := s.quad(4)) is not None:
                        act.wait_ge(values_done, n4)
                    act.wait_ge(turned, n)
                    copy(e_t[:, b].rearrange("p a b -> p (a b)"), ps_t[b][:, :]).then_inc(turned_copied, 1)
                if (n := s.quad(0)) is not None:
                    if (n2 := s.quad(2)) is not None:
                        act.wait_ge(turned, n2)
                    if s.i == 0 and (n2 := s.phase(2)) is not None:
                        act.wait_ge(recip_done, n2)
                    act.wait_ge(biased, n)
                    for h in range(TH):
                        at = TH * s.i + h
                        last = act.activation(e_sb[:, b, h, :], neg_a[:, b, h, :], ACT.Exp, scale=-1.0,
                                              bias=neg_max[:, s.t % 2, at:at + 1],
                                              accum_out=sums[:, s.t % 2, at:at + 1])
                    last.then_inc(exp_done, 1)
                c = s.r16 - SPLIT_AT
                if 0 <= c < CH and s.group(2) is not None:
                    g = s.r // SPG
                    if c == 0:
                        act.wait_ge(made["q"], s.times(PAIR * TILES, TILES * (g + 1)))
                    act.wait_ge(xt_loaded, s.times(16 * PAIR * CH, 16 * (CH * g + c + 1)))
                    copy(xt_hi[:, s.par, c, :], xt_raw[:, :]).then_inc(xt_hi_done, 1)
                if s.i == 2 and (n := s.phase(1)) is not None:
                    f = s.r // GG - 1
                    g, t = f // TILES, f % TILES
                    free = s._count(PAIR * GG, GG * (g if t else g - 1), GRAPHS)
                    if free is not None:
                        act.wait_ge(made["o"], free)
                    act.wait_ge(o_done, n)
                    copy(o_hi[:, o_slot(t, g % PAIR), :], ro_t[:, :]).then_inc(o_hi_done, 1)
                if s.i == 1 and (n := s.phase(1)) is not None:
                    if (n2 := s.phase(2)) is not None:
                        act.wait_ge(o_lo_done, n2)
                    act.wait_ge(r_turned, n)
                    copy(ro_t[:, :], ps_r[:, :]).then_inc(r_copied, 1)

            iterations(act, step)

        @block.vector
        def _(dve):
            def rest(out, whole, hi):
                return dve.tensor_tensor(out, whole, hi.bitcast(F32), ALU.subtract)

            def x_lo(par, c, n, whole):
                dve.wait_ge(xt_hi_done, n)
                rest(xt_lo[:, par, c, :], whole, xt_hi[:, par, c, :]).then_inc(xt_lo_done, 1)

            def double_adj(par):
                adj = adj_sb[:, par].rearrange("p a b -> p (a b)")
                dve.tensor_scalar(adj, adj, 2.0, None, ALU.mult).then_inc(adj_done, 1)

            def take_lo(kind, index, n, in_, later):
                if kind == "q":
                    dve.wait_ge(q_hi_done, n)
                    dve.scalar_tensor_tensor(out=q_lo[:, index % 2, :], in0=in_, scalar=SCALE,
                                             in1=q_hi[:, index % 2, :].bitcast(F32), op0=ALU.mult,
                                             op1=ALU.subtract).then_inc(q_lo_done, 1)
                elif kind == "k":
                    if later:
                        dve.wait_ge(kd_done, n - 1)
                    dve.wait_ge(k_hi_done, n)
                    rest(k_lo[:, :], in_, k_hi[:, :]).then_inc(k_lo_done, 1)

            def weight_lo(kind, c):
                dve.wait_ge(w_hi_done, CH * ORDER.index(kind) + c + 1)
                w = WEIGHT[kind]
                rest(w_lo[:, w, c, :], w_stage[kind][:, c], w_hi[:, w, c, :]).then_inc(w_lo_done, 1)

            dve.memset(kd_lo[:, :, :, :].bitcast(F32), 0.0).then_inc(zeroed, 1)
            for c in range(CH):
                x_lo(0, c, c + 1, xt_stage[0, c])
                weight_lo("k", c)
            for c in range(CH):
                weight_lo("q", c)
            take_lo("k", 0, 1, ps_w[1][:, :], False)
            for c in range(CH):
                weight_lo("v", c)
            take_lo("q", 0, 1, ps_w[0][:, :], False)
            for c in range(CH):
                x_lo(1, c, CH + c + 1, xt_stage[1, c])
            for c in range(CH):
                weight_lo("o", c)
            dve.wait_ge(adj_loaded[0], 16)
            double_adj(0)

            def step(s):
                b = s.r % 2
                g = s.r // SPG
                c = s.r16 - SPLIT_AT - 1
                if 0 <= c < CH and s.group(2) is not None:
                    x_lo(s.par, c, s.times(PAIR * CH, CH * (g + 2) + c + 1), xt_raw[:, :])
                if s.i == 3 and (n := s.phase(1)) is not None:
                    f = s.r // GG - 1
                    slot = o_slot(f % TILES, (f // TILES) % PAIR)
                    dve.wait_ge(o_hi_done, n)
                    rest(o_lo[:, slot, :], ro_t[:, :], o_hi[:, slot, :]).then_inc(o_lo_done, 1)
                if s.i == 2 and (n := s.phase(1)) is not None:
                    dve.wait_ge(values_done, s.quad(3))
                    dve.wait_ge(r_copied, n)
                    dve.scalar_tensor_tensor(out=ro_t[:, :], in0=ps_o[:, :], scalar=BIG, in1=ro_t[:, :],
                                             op0=ALU.min, op1=ALU.mult).then_inc(o_done, 1)
                if (n := s.quad(0)) is not None:
                    dve.wait_ge(scores_done, n)
                    if s.r16 == 0:
                        dve.wait_ge(adj_done, s.group(0))
                    if (n2 := s.quad(2)) is not None:
                        dve.wait_ge(exp_done, n2)
                aggr = (p := s.product(3)) is not None and p[0] == "o"
                if aggr:
                    dve.wait_ge(stats_done, p[3])
                if (n := s.quad(1)) is not None:
                    dve.wait_ge(biased, n)
                    t1, i1 = ((s.r - 1) // GG) % 2, (s.r - 1) % GG
                    dve.tensor_reduce(neg_min[:, t1, TH * i1:TH * (i1 + 1)], neg_a[:, 1 - b], AX.X,
                                      ALU.max).then_inc(min_done, 1)
                if s.i == 0 and (n := s.phase(1)) is not None:
                    t1 = (s.r // GG - 1) % 2
                    if (n2 := s.phase(2)) is not None:
                        dve.wait_ge(r_done, n2)
                    dve.wait_ge(min_done, s.quad(1))
                    dve.scalar_tensor_tensor(out=abs_max[:, :], in0=neg_max[:, t1, :], scalar=-1.0,
                                             in1=neg_min[:, t1, :], op0=ALU.mult, op1=ALU.max).then_inc(abs_done, 1)
                    if (n2 := s.phase(2)) is not None:
                        dve.wait_ge(r_wide_done, n2)
                    dve.wait_ge(exp_done, s.quad(1))
                    dve.reciprocal(r_inv[:, :], sums[:, t1, :]).then_inc(recip_done, 1)
                    dve.wait_ge(abs_done, n)
                    dve.tensor_scalar(abs_max[:, :], abs_max[:, :], 0.0, None, ALU.is_gt).then_inc(nonzero_done, 1)
                    dve.wait_ge(nonzero_done, n)
                    dve.wait_ge(recip_done, n)
                    dve.scalar_tensor_tensor(out=r_inv[:, :], in0=r_inv[:, :], scalar=0.0, in1=abs_max[:, :],
                                             op0=ALU.max, op1=ALU.mult).then_inc(r_done, 1)
                if aggr:
                    dve.bn_aggr(mean_var[:, p[1], :], ln_stats[:, :]).then_inc(mean_done, 1)
                if s.quad(0) is not None:
                    for h in range(TH):
                        at = TH * s.i + h
                        last = dve.tensor_tensor_reduce(
                            out=neg_a[:, b, h, :], in0=ps_s[b][:, h * NODES:(h + 1) * NODES],
                            in1=adj_sb[:, s.par, s.i, :], scale=-1.0, scalar=INF, op0=ALU.add, op1=ALU.min,
                            accum_out=neg_max[:, s.t % 2, at:at + 1])
                    last.then_inc(biased, 1)
                if (p := s.product(1)) is not None:
                    kind, index, par, n = p
                    if kind == "o":
                        if index == 0:
                            dve.wait_ge(x_loaded, s.times(16 * PAIR, 16 * ((s.r - 1) // SPG)))
                        dve.wait_ge(made["o"], n)
                        row = x_sb[:, index, :]
                        dve.tensor_tensor(row, ps_w[1 - b][:, :], row, ALU.add).then_inc(added, 1)
                    else:
                        take_lo(kind, index, n, ps_w[1 - b][:, :], True)
                if (p := s.product(2)) is not None and p[0] == "o":
                    n = p[3]
                    dve.wait_ge(added, n)
                    if not (isinstance(n, int) and n == 1):
                        dve.wait_ge(mean_done, n - 1)
                    dve.bn_stats(ln_stats[:, :], x_sb[:, p[1], :]).then_inc(stats_done, 1)
                if (p := s.product(LN_LAG)) is not None and p[0] == "o":
                    dve.wait_ge(rstd_done, p[3])
                    row = x_sb[:, p[1], :]
                    dve.tensor_scalar(row, row, mean_var[:, p[1], 0:1], rstd[:, p[1]:p[1] + 1], ALU.subtract,
                                      ALU.mult).then_inc(normed, 1)
                if s.r16 == SPLIT_AT and s.group(1) is not None:
                    dve.wait_ge(adj_loaded[1 - s.par], s.times(16, 16 * (s.par + 1)))
                    double_adj(1 - s.par)

            iterations(dve, step)


def kernel(x, adj, L0_gnn_Wq, L0_gnn_Wk, L0_gnn_Wv, L0_gnn_Wo):
    import numpy as np
    import concourse.bacc as bacc
    from concourse.bass_utils import run_bass_kernel_spmd

    x, adj = np.asarray(x), np.asarray(adj)

    def turned(w):
        return np.ascontiguousarray(np.asarray(w).T.reshape(CH, P, D).transpose(1, 0, 2))

    xg = x.reshape(GROUPS, GG, NODES, D)
    arrays = {
        "xt": np.ascontiguousarray(xg.reshape(GROUPS, GG * NODES, CH, P).transpose(0, 2, 3, 1)),
        "x": np.ascontiguousarray(xg.transpose(0, 2, 1, 3)),
        "adj": np.ascontiguousarray(adj.reshape(GROUPS, GG, NODES, NODES).transpose(0, 2, 1, 3)),
        "wq": turned(L0_gnn_Wq),
        "wk": turned(L0_gnn_Wk),
        "wv": turned(L0_gnn_Wv),
        "wo": turned(L0_gnn_Wo),
    }
    nc = bacc.Bacc("TRN2", target_bir_lowering=False, num_devices=1)
    aps = [nc.dram_tensor(name, a.shape, F32, kind="ExternalInput").ap() for name, a in arrays.items()]
    out = nc.dram_tensor("out", [GROUPS, NODES, GG, D], F32, kind="ExternalOutput").ap()
    build(nc, *aps, out)
    r = run_bass_kernel_spmd(nc, [arrays], core_ids=[0])
    got = r.results[0]["out"]
    return np.ascontiguousarray(got.transpose(0, 2, 1, 3)).reshape(GRAPHS, NODES, D)
```

```python
from contextlib import ExitStack

import concourse.bass as bass
from concourse import mybir

F32 = mybir.dt.float32
F32R = mybir.dt.float32r
ALU = mybir.AluOpType
ACT = mybir.ActivationFunctionType
AX = mybir.AxisListType

P = 128
GRAPHS = 128
NODES = 128
D = 512
HEADS = 16
HD = D // HEADS
CH = D // P
TILES = CH
TH = HEADS // TILES
PAIRS = TH // 2
HALF = P // 2
EARLY_TILES = 2
GG = 4
GROUPS = GRAPHS // GG
SPG = TILES * GG
PAIR = 2
STEPS = PAIR * SPG
ITERS = GROUPS // PAIR
SCALE = float(D) ** -0.5
EPS = 1e-5
BIG = 3.0e38
INF = float("inf")

PLAN = [("q", 1, 0), ("v", 0, 1), ("v", 1, 1), ("k", 2, 0),
        ("q", 2, 0), ("o", 0, -1), ("o", 1, -1), ("k", 3, 0),
        ("q", 3, 0), ("o", 2, -1), ("v", 2, 1), ("k", 0, 1),
        ("q", 0, 1), ("o", 3, -1), ("v", 3, 1), ("k", 1, 1)]
FIRST_PLAN = [("q", 1, 0), ("v", 2, 0), ("v", 3, 0), ("k", 2, 0), ("q", 2, 0), ("v", 0, 1), ("v", 1, 1)] + PLAN[7:]
LAST_PLAN = [("q", 1, 0), None, None, ("k", 2, 0), ("q", 2, 0), ("o", 0, -1), ("o", 1, -1), ("k", 3, 0),
             ("q", 3, 0), ("o", 2, -1), ("o", 3, -1), None, None, None, None, None]
DRAIN_PLAN = [None] * 3 + [("o", 0, -1), ("o", 1, -1), ("o", 2, -1), ("o", 3, -1)] + [None] * 9
FIRST = [("k", 0), ("q", 0), ("v", 0), ("v", 1), ("k", 1)]
BEFORE_PLAN = [None] * 11 + [("k", 0, 1), ("q", 0, 1), ("v", 0, 1), ("v", 1, 1), ("k", 1, 1)]
ORDER = "kqvo"
WEIGHT = {"q": 0, "k": 1, "v": 2, "o": 3}
SPLIT_STEPS = (9, 11, 13, 14)
ADJ_AT = 2
LN_LAG = 5
DRAIN = 6 + LN_LAG + 1


class Step:

    def __init__(self, m, r):
        self.m, self.r = m, r
        self.r16 = r % SPG
        self.par = (r // SPG) % PAIR
        self.t = self.r16 // GG
        self.i = r % GG

    def times(self, per, const):
        return self.m * per + const

    def _count(self, per, const, most):
        n = self.m * per + const
        if isinstance(self.m, int) and not 0 < n <= most:
            return None
        return n

    def quad(self, lag):
        return self._count(STEPS, self.r - lag + 1, GROUPS * SPG)

    def phase(self, lag):
        return self._count(PAIR * TILES, self.r // GG - lag + 1, GROUPS * TILES)

    def group(self, ahead):
        return self._count(PAIR, self.r // SPG + ahead + 1, GROUPS)

    def product(self, lag):
        r = self.r - lag
        plan = PLAN
        if isinstance(self.m, int) and self.m == 0 and r < SPG:
            plan = BEFORE_PLAN if r < 0 else FIRST_PLAN
        if isinstance(self.m, int) and self.m == ITERS - 1 and r // SPG >= PAIR - 1:
            plan = LAST_PLAN if r // SPG == PAIR - 1 else DRAIN_PLAN
        if plan[r % SPG] is None:
            return None
        kind, index, ahead = plan[r % SPG]
        g = r // SPG + ahead
        n = self._count(PAIR * GG, GG * g + index + 1, GRAPHS)
        return None if n is None else (kind, index, g % PAIR, n)


def o_slot(tile, par):
    return tile + TILES if par and tile < EARLY_TILES else tile


def build(nc, xt_d, x_d, adj_d, wq_d, wk_d, wv_d, wo_d, out_d):
    ctx = ExitStack()
    with ctx:
        def sb(name, shape, dt=F32):
            return ctx.enter_context(nc.sbuf_tensor(name, shape, dt))

        def bank(name):
            return ctx.enter_context(nc.psum_tensor(name, [P, 512], F32))

        def sem(name):
            return ctx.enter_context(nc.semaphore(name))

        w_hi = sb("w_hi", [P, 4, CH, D], F32R)
        w_lo = sb("w_lo", [P, 4, CH, D], F32R)
        xt_raw = sb("xt_raw", [P, 2, 512])
        xt_hi = sb("xt_hi", [P, PAIR, CH, 512], F32R)
        xt_lo = sb("xt_lo", [P, PAIR, CH, 512], F32R)
        q_hi = sb("q_hi", [P, 2, PAIRS, 512], F32R)
        q_mix = sb("q_mix", [P, 2, PAIRS, 512], F32R)
        k_hi = sb("k_hi", [P, 512], F32R)
        k_lo = sb("k_lo", [P, 512], F32R)
        k_mix = sb("k_mix", [P, 2, GG, PAIRS, 2 * NODES], F32R)
        v_sb = sb("v_sb", [P, PAIR, GG, D])
        x_sb = sb("x_sb", [P, GG, D])
        adj_sb = sb("adj_sb", [P, PAIR, GG, NODES])
        neg_a = sb("neg_a", [P, 2, TH, NODES])
        e_sb = sb("e_sb", [P, 2, TH, NODES])
        e_t = sb("e_t", [P, 2, TH, NODES])
        o_hi = sb("o_hi", [P, TILES + EARLY_TILES, 512], F32R)
        o_lo = sb("o_lo", [P, TILES + EARLY_TILES, 512], F32R)
        ident = sb("ident", [P, P])
        constants = sb("constants", [P, 5])
        ones, eps, minus_half, one_and_half, minus_one = (constants[:, c:c + 1] for c in range(5))
        neg_max = sb("neg_max", [P, 2, TH])
        neg_min = sb("neg_min", [P, 2, TH])
        sums = sb("sums", [P, 2, TH])
        recip = sb("recip", [P, 2, TH])
        abs_max = sb("abs_max", [P, 2, TH])
        nonzero = sb("nonzero", [P, 2, TH])
        r_inv = sb("r_inv", [P, 2, TH])
        ln_stats = sb("ln_stats", [P, 6])
        mean_var = sb("mean_var", [P, GG, 2])
        ln_tmp = sb("ln_tmp", [P, 7])
        rstd = sb("rstd", [P, GG])
        shift = sb("shift", [P, GG])

        ps_w = [bank("ps_w0"), bank("ps_w1")]
        ps_s = [bank("ps_s0"), bank("ps_s1")]
        ps_t = [bank("ps_t0"), bank("ps_t1")]
        ps_o = [bank("ps_o0"), bank("ps_o1")]

        consts = sem("consts")
        CONSTS = 7
        zeroed = sem("zeroed")
        w_loaded = {(kind, c): sem(f"w{kind}_loaded{c}") for kind in ORDER for c in range(CH)}
        w_hi_done = sem("w_hi_done")
        w_lo_done = sem("w_lo_done")
        xt_staged = {(g, c): sem(f"xt_staged{g}{c}") for g in range(PAIR) for c in range(CH)}
        xt_loaded = [sem(f"xt_loaded{n}") for n in range(2)]
        x_loaded = sem("x_loaded")
        adj_loaded = [sem(f"adj_loaded{n}") for n in range(PAIR)]
        adj_done = sem("adj_done")
        xt_hi_done = sem("xt_hi_done")
        xt_lo_done = sem("xt_lo_done")
        made = {kind: sem(f"{kind}_made") for kind in "qkvo"}
        v_copied = sem("v_copied")
        q_hi_done = sem("q_hi_done")
        q_lo_done = sem("q_lo_done")
        k_hi_done = sem("k_hi_done")
        k_lo_done = sem("k_lo_done")
        k_mixed = sem("k_mixed")
        q_mixed = sem("q_mixed")
        scores_done = sem("scores_done")
        biased = sem("biased")
        min_done = sem("min_done")
        exp_done = sem("exp_done")
        turned = sem("turned")
        turned_copied = sem("turned_copied")
        values_done = sem("values_done")
        abs_done = sem("abs_done")
        nonzero_done = sem("nonzero_done")
        recip_done = sem("recip_done")
        r_done = sem("r_done")
        normalised = sem("normalised")
        o_hi_done = sem("o_hi_done")
        o_lo_done = sem("o_lo_done")
        added = sem("added")
        stats_done = sem("stats_done")
        mean_done = sem("mean_done")
        pool_step = sem("pool_step")
        rstd_done = sem("rstd_done")
        normed = sem("normed")
        stored = sem("stored")

        def iterations(eng, step):
            for r in range(STEPS):
                step(Step(0, r))
            with eng.Fori(1, ITERS - 1) as m:
                for r in range(STEPS):
                    step(Step(m, r))
            for r in range(STEPS + DRAIN):
                step(Step(ITERS - 1, r))

        w_stage = {"k": v_sb[:, 1], "q": x_sb[:, :, :], "v": v_sb[:, 0], "o": v_sb[:, 1]}
        xt_stage = {(g, c): buffer[:, c % 2].rearrange("p a b -> p (a b)")
                    for g, c, buffer in ((0, 0, neg_a), (0, 1, neg_a), (0, 2, e_sb), (0, 3, e_sb),
                                         (1, 0, e_t), (1, 1, e_t))}
        xt_stage[1, 2] = xt_raw[:, 0, :]
        xt_stage[1, 3] = xt_raw[:, 1, :]

        block = ctx.enter_context(nc.Block())

        @block.sync
        def _(sp):
            def stage_w(kind, c):
                sp.dma_start(w_stage[kind][:, c], {"q": wq_d, "k": wk_d, "v": wv_d, "o": wo_d}[kind][:, c]
                             ).then_inc(w_loaded[kind, c], 16)

            def stage_chunk(g, c):
                sp.dma_start(xt_stage[g, c], xt_d[g, c]).then_inc(xt_staged[g, c], 16)

            for c in range(CH):
                stage_chunk(0, c)
                stage_w("k", c)
            for c in range(CH):
                stage_w("q", c)
            for c in range(CH):
                stage_w("v", c)
            sp.dma_start(adj_sb[:, 0], adj_d[0]).then_inc(adj_loaded[0], 16)
            for c in range(CH):
                stage_chunk(1, c)
            for c in range(CH):
                if c == 0:
                    sp.wait_ge(w_hi_done, CH)
                    sp.wait_ge(w_lo_done, CH)
                stage_w("o", c)

            def step(s):
                g = s.r // SPG
                for c in range(CH):
                    if s.r16 == (0 if c < 2 else SPLIT_STEPS[c - 2] + 2) and (n := s.group(2)) is not None:
                        before = s.times(PAIR * CH, CH * (g + 2) + c - 1)
                        sp.wait_ge(xt_hi_done, before)
                        sp.wait_ge(xt_lo_done, before)
                        sp.dma_start(xt_raw[:, c % 2, :], xt_d[n - 1, c]).then_inc(xt_loaded[c % 2], 16)
                if s.r16 == 0 and (n := s.group(1)) is not None:
                    if (n1 := s.quad(1)) is not None:
                        sp.wait_ge(biased, n1)
                    sp.dma_start(adj_sb[:, 1 - s.par], adj_d[n - 1]).then_inc(adj_loaded[1 - s.par], 16)
                if (p := s.product(LN_LAG)) is not None and p[0] == "o":
                    sp.wait_ge(normed, p[3])
                    sp.dma_start(out_d[s.times(PAIR, (s.r - LN_LAG) // SPG - 1), :, p[1], :],
                                 x_sb[:, p[1], :]).then_inc(stored, 16)
                if s.r16 == 3 and (n := s.group(-1)) is not None:
                    if s.group(-2) is not None:
                        sp.wait_ge(stored, s.times(16 * GG * PAIR, 16 * GG * (g - 1)))
                    sp.dma_start(x_sb[:, :, :], x_d[n - 1]).then_inc(x_loaded, 16)

            sp.wait_ge(w_hi_done, 2 * CH)
            sp.wait_ge(w_lo_done, 2 * CH)
            iterations(sp, step)
            sp.wait_ge(stored, 16 * GRAPHS)

        @block.gpsimd
        def _(pool):
            pool.memset(ident[:, :], 0.0).then_inc(consts, 1)
            pool.memset(ones, 1.0).then_inc(consts, 1)
            pool.memset(eps, EPS).then_inc(consts, 1)
            pool.memset(minus_half, -0.5).then_inc(consts, 1)
            pool.memset(one_and_half, 1.5).then_inc(consts, 1)
            pool.memset(minus_one, -1.0).then_inc(consts, 1)
            pool.memset(q_hi[:, :, :, :].bitcast(F32), 0.0).then_inc(zeroed, 1)
            pool.memset(k_mix[:, 0].bitcast(F32), 0.0).then_inc(zeroed, 1)
            pool.wait_ge(consts, 6)
            pool.affine_select(out=ident[:, :], in_=ident[:, :], compare_op=ALU.not_equal, fill=1.0,
                               base=0, pattern=[[-1, P]], channel_multiplier=1).then_inc(consts, 1)

            def place(parts):
                for n, (out, in_) in enumerate(parts):
                    in_ = in_.bitcast(F32).rearrange("p (g n) -> p g n", g=GG)
                    if n == 0:
                        one = constants[0:HD, 0:1]
                        pool.tensor_tensor(out, in_, one.unsqueeze(2).to_broadcast([HD, GG, NODES]), ALU.mult)
                    else:
                        last = pool.tensor_scalar(out, in_, 1.0, 0.0, ALU.mult, ALU.add)
                return last

            def mix_k(slot):
                parts = []
                for p in range(PAIRS):
                    for j in range(2):
                        home = HALF * p + HD * j
                        away = HALF * (1 - p) + HD * j
                        cols = slice(j * NODES, (j + 1) * NODES)
                        parts.append((k_mix[home:home + HD, slot, :, p, cols], k_hi[home:home + HD, :]))
                        parts.append((k_mix[away:away + HD, slot, :, p, cols], k_lo[home:home + HD, :]))
                place(parts).then_inc(k_mixed, 1)

            def mix_q(slot):
                parts = []
                for p in range(PAIRS):
                    for j in range(2):
                        home = HALF * p + HD * j
                        away = HALF * (1 - p) + HD * j
                        parts.append((q_mix[away:away + HD, slot, p, :].rearrange("p (g n) -> p g n", g=GG),
                                      q_hi[home:home + HD, slot, p, :]))
                place(parts).then_inc(q_mixed, 1)

            pool.wait_ge(zeroed, 3)
            pool.wait_ge(consts, CONSTS)
            pool.wait_ge(k_hi_done, 1)
            pool.wait_ge(k_lo_done, 1)
            mix_k(0)
            pool.wait_ge(q_hi_done, 1)
            mix_q(0)

            def latest(s, kind, lag):
                for more in range(lag, lag + 2 * SPG):
                    if (p := s.product(more)) is not None and p[0] == kind:
                        return p[3]

            def step(s):
                g = s.r // SPG

                def parts_placed(lag):
                    pool.wait_ge(k_mixed, latest(s, "k", lag))
                    pool.wait_ge(q_mixed, latest(s, "q", lag))

                def wide_done():
                    split = s.times(PAIR * CH, CH * (g + 2) + sum(at + 1 <= s.r16 for at in SPLIT_STEPS))
                    pool.wait_ge(xt_lo_done, min(split, CH * GROUPS) if isinstance(split, int) else split)
                    if (n1 := latest(s, "o", 4)) is not None:
                        pool.wait_ge(rstd_done, n1)

                if s.r16 - 1 in SPLIT_STEPS and s.group(2) is not None:
                    c = SPLIT_STEPS.index(s.r16 - 1)
                    n = s.times(PAIR * CH, CH * (g + 2) + c + 1)
                    parts_placed(2)
                    pool.wait_ge(xt_hi_done, n)
                    pool.tensor_tensor(xt_lo[:, s.par, c, :], xt_raw[:, c % 2, :],
                                       xt_hi[:, s.par, c, :].bitcast(F32), ALU.subtract).then_inc(xt_lo_done, 1)
                if (p := s.product(1)) is not None and p[0] == "k":
                    pool.wait_ge(k_hi_done, p[3])
                    pool.wait_ge(k_lo_done, p[3])
                    if (n1 := s.quad(1)) is not None:
                        pool.wait_ge(scores_done, n1)
                    wide_done()
                    mix_k(p[1] % 2)
                if (p := s.product(1)) is not None and p[0] == "q":
                    pool.wait_ge(q_hi_done, p[3])
                    wide_done()
                    mix_q(p[1] % 2)
                if (p := s.product(3)) is not None and p[0] == "o":
                    i = p[1]
                    ve, minus_mean, y, vy, vyy, half, rest = (ln_tmp[:, c:c + 1] for c in range(7))
                    before = GG * ((s.r - 3) // SPG - 1) + i

                    def own(c):
                        pool.wait_ge(pool_step, s.times(8 * PAIR * GG, 8 * before + c))

                    parts_placed(1)
                    if not (isinstance(p[3], int) and p[3] == 1):
                        pool.wait_ge(rstd_done, p[3] - 1)
                    pool.wait_ge(mean_done, p[3])
                    pool.tensor_tensor(ve, mean_var[:, i, 1:2], eps, ALU.add).then_inc(pool_step, 1)
                    pool.tensor_tensor(minus_mean, mean_var[:, i, 0:1], minus_one, ALU.mult).then_inc(pool_step, 1)
                    own(1)
                    pool.tensor_tensor(y, ve, minus_half, ALU.pow).then_inc(pool_step, 1)
                    own(3)
                    pool.tensor_tensor(vy, ve, y, ALU.mult).then_inc(pool_step, 1)
                    own(4)
                    pool.tensor_tensor(vyy, vy, y, ALU.mult).then_inc(pool_step, 1)
                    own(5)
                    pool.tensor_tensor(half, vyy, minus_half, ALU.mult).then_inc(pool_step, 1)
                    own(6)
                    pool.tensor_tensor(rest, half, one_and_half, ALU.add).then_inc(pool_step, 1)
                    own(7)
                    pool.tensor_tensor(rstd[:, i:i + 1], y, rest, ALU.mult).then_inc(pool_step, 1)
                    own(8)
                    pool.tensor_tensor(shift[:, i:i + 1], minus_mean, rstd[:, i:i + 1], ALU.mult).then_inc(rstd_done, 1)

            iterations(pool, step)

        @block.tensor
        def _(pe):
            def split_product(out, chunks, lhs_hi, lhs_lo, rhs_hi, rhs_lo, before=None):
                for c in range(chunks):
                    if before:
                        before(c)
                    pe.matmul(out, lhs_lo(c), rhs_hi(c), start=(c == 0), stop=False)
                    pe.matmul(out, lhs_hi(c), rhs_lo(c), start=False, stop=False)
                for c in range(chunks):
                    last = pe.matmul(out, lhs_hi(c), rhs_hi(c), start=False, stop=(c == chunks - 1))
                return last

            def weight_product(kind, index, par, out, before=None):
                w, cols = WEIGHT[kind], slice(index * P, (index + 1) * P)
                if kind in "qk":
                    last = split_product(out, CH, lambda c: w_hi[:, w, c, cols], lambda c: w_lo[:, w, c, cols],
                                         lambda c: xt_hi[:, par, c, :], lambda c: xt_lo[:, par, c, :], before)
                elif kind == "v":
                    last = split_product(out, CH, lambda c: xt_hi[:, par, c, cols], lambda c: xt_lo[:, par, c, cols],
                                         lambda c: w_hi[:, w, c, :], lambda c: w_lo[:, w, c, :], before)
                else:
                    last = split_product(out, CH, lambda c: o_hi[:, o_slot(c, par), cols],
                                         lambda c: o_lo[:, o_slot(c, par), cols],
                                         lambda c: w_hi[:, w, c, :], lambda c: w_lo[:, w, c, :], before)
                last.then_inc(made[kind], 1)

            released = {"v": v_copied, "k": k_lo_done, "q": q_lo_done, "o": added}

            for u, (kind, index) in enumerate(FIRST):
                def before(c):
                    n = CH * ORDER.index(kind) + c + 1
                    if kind == "k":
                        pe.wait_ge(xt_hi_done, c + 1)
                        pe.wait_ge(xt_lo_done, c + 1)
                    pe.wait_ge(w_hi_done, n)
                    pe.wait_ge(w_lo_done, n)
                if u >= 2:
                    k2, i2 = FIRST[u - 2]
                    pe.wait_ge(released[k2], i2 + 1)
                weight_product(kind, index, 0, ps_w[(u + 1) % 2][:, :], before if index == 0 else None)
            pe.wait_ge(consts, CONSTS)

            def step(s):
                b = s.r % 2
                if s.quad(0) is not None:
                    if s.i == 0:
                        pe.wait_ge(k_mixed, s.phase(0))
                        pe.wait_ge(q_mixed, s.phase(0))
                        pe.wait_ge(q_lo_done, s.phase(0))
                    if (n := s.quad(2)) is not None:
                        pe.wait_ge(biased, n)
                    slot, nodes = s.t % 2, slice(s.i * NODES, (s.i + 1) * NODES)
                    for p in range(PAIRS):
                        out = ps_s[b][:, p * 2 * NODES:(p + 1) * 2 * NODES]
                        pe.matmul(out, q_mix[:, slot, p, nodes], k_mix[:, slot, s.i, p, :], start=True, stop=False)
                        last = pe.matmul(out, q_hi[:, slot, p, nodes], k_mix[:, slot, s.i, p, :], start=False,
                                         stop=True)
                    last.then_inc(scores_done, 1)
                if (n := s.quad(2)) is not None:
                    if (n4 := s.quad(4)) is not None:
                        pe.wait_ge(turned_copied, n4)
                    pe.wait_ge(normalised, n)
                    for h in range(TH):
                        last = pe.transpose(ps_t[b][:, h * P:(h + 1) * P], e_sb[:, b, h, :], ident[:, :])
                    last.then_inc(turned, 1)
                if (p := s.product(0)) is not None:
                    kind, index, par, n = p
                    for lag in range(2, SPG, 2):
                        if (p2 := s.product(lag)) is not None:
                            pe.wait_ge(released[p2[0]], p2[3])
                            break
                    if kind == "v" and index == 0:
                        pe.wait_ge(xt_hi_done, s.times(PAIR * CH, CH * (s.r // SPG + 2)))
                        pe.wait_ge(xt_lo_done, s.times(PAIR * CH, CH * (s.r // SPG + 2)))
                    if kind == "o" and index == 0:
                        if not isinstance(s.m, int) or s.m == 0:
                            pe.wait_ge(w_hi_done, 4 * CH)
                            pe.wait_ge(w_lo_done, 4 * CH)
                        pe.wait_ge(o_hi_done, s.times(PAIR * TILES, TILES * (s.r // SPG)))
                        pe.wait_ge(o_lo_done, s.times(PAIR * TILES, TILES * (s.r // SPG)))
                    weight_product(kind, index, par, ps_w[b][:, :])
                if (n := s.quad(2)) is not None:
                    r2 = s.r - 2
                    par, t, i = (r2 // SPG) % PAIR, (r2 % SPG) // GG, r2 % GG
                    if r2 % SPG < GG:
                        pe.wait_ge(v_copied, s.times(PAIR * GG, GG * (r2 // SPG) + i + 1))
                    if i == 0 and (n1 := s.phase(2)) is not None:
                        pe.wait_ge(o_lo_done, n1)
                    pe.wait_ge(turned_copied, n)
                    for h in range(TH):
                        cols = slice((TH * t + h) * HD, (TH * t + h + 1) * HD)
                        out = ps_o[(r2 // GG) % 2][HD * h:HD * (h + 1), i * P:(i + 1) * P]
                        last = pe.matmul(out, v_sb[:, par, i, cols], e_t[:, b, h, :], start=True, stop=True)
                    last.then_inc(values_done, 1)

            iterations(pe, step)

        @block.scalar
        def _(act):
            def copy(out, in_, scale=1.0):
                return act.activation(out, in_, ACT.Copy, scale=scale)

            def take(kind, index, par, n, in_, later):
                act.wait_ge(made[kind], n)
                if kind == "v":
                    copy(v_sb[:, par, index, :], in_).then_inc(v_copied, 1)
                elif kind == "q":
                    for p in range(PAIRS):
                        rows = slice(HALF * p, HALF * (p + 1))
                        last = copy(q_hi[rows, index % 2, p, :], in_[rows, :], SCALE)
                    last.then_inc(q_hi_done, 1)
                elif kind == "k":
                    if later:
                        act.wait_ge(k_mixed, n - 1)
                    copy(k_hi[:, :], in_).then_inc(k_hi_done, 1)

            def weight_hi(kind, c):
                act.wait_ge(w_loaded[kind, c], 16)
                copy(w_hi[:, WEIGHT[kind], c, :], w_stage[kind][:, c]).then_inc(w_hi_done, 1)

            def staged_hi(g, c):
                act.wait_ge(xt_staged[g, c], 16)
                copy(xt_hi[:, g, c, :], xt_stage[g, c]).then_inc(xt_hi_done, 1)

            def first(u):
                kind, index = FIRST[u]
                take(kind, index, 0, index + 1, ps_w[(u + 1) % 2][:, :], False)

            for c in range(CH):
                staged_hi(0, c)
                weight_hi("k", c)
            for c in range(CH):
                weight_hi("q", c)
            first(0)
            for c in range(CH):
                weight_hi("v", c)
            act.wait_ge(zeroed, 3)
            first(1)
            first(2)
            for c in range(CH):
                staged_hi(1, c)
            first(3)
            for c in range(CH):
                weight_hi("o", c)

            def step(s):
                b = s.r % 2
                if (p := s.product(1)) is not None and p[0] != "o":
                    kind, index, par, n = p
                    if isinstance(s.m, int) and s.m == 0 and (kind, par, index) == ("v", 1, 0):
                        act.wait_ge(w_lo_done, 4 * CH)
                    take(kind, index, par, n, ps_w[1 - b][:, :], True)
                if (n := s.quad(2)) is not None:
                    if (n4 := s.quad(4)) is not None:
                        act.wait_ge(values_done, n4)
                    act.wait_ge(turned, n)
                    copy(e_t[:, b].rearrange("p a b -> p (a b)"), ps_t[b][:, :]).then_inc(turned_copied, 1)
                if s.i == 2 and (n := s.phase(1)) is not None:
                    f = s.r // GG - 1
                    g, t = f // TILES, f % TILES
                    free = s._count(PAIR * GG, GG * (g - 1 if t < EARLY_TILES else g), GRAPHS)
                    if free is not None:
                        act.wait_ge(made["o"], free)
                    act.wait_ge(values_done, s.quad(3))
                    copy(o_hi[:, o_slot(t, g % PAIR), :], ps_o[f % 2][:, :]).then_inc(o_hi_done, 1)

                if (n := s.quad(0)) is not None:
                    if (n2 := s.quad(2)) is not None:
                        act.wait_ge(turned, n2)
                    act.wait_ge(biased, n)
                    for h in range(TH):
                        last = act.activation(e_sb[:, b, h, :], neg_a[:, b, h, :], ACT.Exp, scale=-1.0,
                                              bias=neg_max[:, b, h:h + 1],
                                              accum_out=sums[:, b, h:h + 1])
                    last.then_inc(exp_done, 1)
                if s.r16 in SPLIT_STEPS and s.group(2) is not None:
                    c = SPLIT_STEPS.index(s.r16)
                    g = s.r // SPG
                    if c == 0:
                        act.wait_ge(made["q"], s.times(PAIR * TILES, TILES * (g + 1)))
                    act.wait_ge(xt_loaded[c % 2], s.times(16 * PAIR * 2, 16 * (2 * g + c // 2 + 1)))
                    copy(xt_hi[:, s.par, c, :], xt_raw[:, c % 2, :]).then_inc(xt_hi_done, 1)
                if (p := s.product(LN_LAG)) is not None and p[0] == "o":
                    act.wait_ge(rstd_done, p[3])
                    row = x_sb[:, p[1], :]
                    act.activation(row, row, ACT.Identity, scale=rstd[:, p[1]:p[1] + 1],
                                   bias=shift[:, p[1]:p[1] + 1]).then_inc(normed, 1)

            iterations(act, step)

        @block.vector
        def _(dve):
            def rest(out, whole, hi):
                return dve.tensor_tensor(out, whole, hi.bitcast(F32), ALU.subtract)

            def x_lo(par, c, n, whole):
                dve.wait_ge(xt_hi_done, n)
                rest(xt_lo[:, par, c, :], whole, xt_hi[:, par, c, :]).then_inc(xt_lo_done, 1)

            def double_adj(par):
                adj = adj_sb[:, par].rearrange("p a b -> p (a b)")
                dve.tensor_scalar(adj, adj, 2.0, None, ALU.mult).then_inc(adj_done, 1)

            def take_lo(kind, index, n, in_, later):
                if kind == "q":
                    dve.wait_ge(q_hi_done, n)
                    for p in range(PAIRS):
                        rows = slice(HALF * p, HALF * (p + 1))
                        last = dve.scalar_tensor_tensor(out=q_mix[rows, index % 2, p, :], in0=in_[rows, :],
                                                        scalar=SCALE, in1=q_hi[rows, index % 2, p, :].bitcast(F32),
                                                        op0=ALU.mult, op1=ALU.subtract)
                    last.then_inc(q_lo_done, 1)
                elif kind == "k":
                    if later:
                        dve.wait_ge(k_mixed, n - 1)
                    dve.wait_ge(k_hi_done, n)
                    rest(k_lo[:, :], in_, k_hi[:, :]).then_inc(k_lo_done, 1)

            def weight_lo(kind, c):
                dve.wait_ge(w_hi_done, CH * ORDER.index(kind) + c + 1)
                w = WEIGHT[kind]
                rest(w_lo[:, w, c, :], w_stage[kind][:, c], w_hi[:, w, c, :]).then_inc(w_lo_done, 1)

            dve.memset(k_mix[:, 1].bitcast(F32), 0.0).then_inc(zeroed, 1)
            for c in range(CH):
                x_lo(0, c, c + 1, xt_stage[0, c])
                weight_lo("k", c)
            for c in range(CH):
                weight_lo("q", c)
            take_lo("k", 0, 1, ps_w[1][:, :], False)
            for c in range(CH):
                weight_lo("v", c)
            take_lo("q", 0, 1, ps_w[0][:, :], False)
            for c in range(CH):
                x_lo(1, c, CH + c + 1, xt_stage[1, c])
            for c in range(CH):
                weight_lo("o", c)
            dve.wait_ge(adj_loaded[0], 16)
            double_adj(0)

            def step(s):
                b = s.r % 2
                g = s.r // SPG
                if (n := s.quad(0)) is not None:
                    dve.wait_ge(scores_done, n)
                    if s.r16 == 0:
                        dve.wait_ge(adj_done, s.group(0))
                    if (n2 := s.quad(2)) is not None:
                        dve.wait_ge(exp_done, n2)
                aggr = (p := s.product(3)) is not None and p[0] == "o"
                if aggr and s.quad(1) is None:
                    dve.wait_ge(stats_done, p[3])
                a = 1 - b

                def bias(h):
                    return dve.tensor_tensor_reduce(
                        out=neg_a[:, b, h, :], in0=ps_s[b][:, h * NODES:(h + 1) * NODES],
                        in1=adj_sb[:, s.par, s.i, :], scale=-1.0, scalar=INF, op0=ALU.add, op1=ALU.min,
                        accum_out=neg_max[:, b, h:h + 1])

                if (n := s.quad(1)) is not None:
                    n3 = s.quad(3)
                    if n3 is not None:
                        dve.wait_ge(abs_done, n3)
                    dve.wait_ge(biased, n)
                    dve.tensor_reduce(neg_min[:, a], neg_a[:, a], AX.X, ALU.max).then_inc(min_done, 1)
                    if n3 is not None:
                        dve.wait_ge(r_done, n3)
                    dve.wait_ge(exp_done, n)
                    if aggr:
                        dve.wait_ge(stats_done, p[3])
                    dve.reciprocal(recip[:, a], sums[:, a]).then_inc(recip_done, 1)
                if s.quad(0) is not None:
                    bias(0)
                if aggr:
                    dve.bn_aggr(mean_var[:, p[1], :], ln_stats[:, :]).then_inc(mean_done, 1)
                if (n := s.quad(1)) is not None:
                    if n3 is not None:
                        dve.wait_ge(nonzero_done, n3)
                    dve.wait_ge(min_done, n)
                    dve.scalar_tensor_tensor(out=abs_max[:, a], in0=neg_max[:, a], scalar=-1.0, in1=neg_min[:, a],
                                             op0=ALU.mult, op1=ALU.max).then_inc(abs_done, 1)
                if s.quad(0) is not None:
                    bias(1)
                if (n := s.quad(1)) is not None:
                    dve.wait_ge(abs_done, n)
                    dve.tensor_scalar(nonzero[:, a], abs_max[:, a], 0.0, None, ALU.is_gt).then_inc(nonzero_done, 1)
                if s.quad(0) is not None:
                    bias(2)
                if (n := s.quad(1)) is not None:
                    if n3 is not None:
                        dve.wait_ge(normalised, n3)
                    dve.wait_ge(nonzero_done, n)
                    dve.wait_ge(recip_done, n)
                    dve.scalar_tensor_tensor(out=r_inv[:, a], in0=recip[:, a], scalar=0.0, in1=nonzero[:, a],
                                             op0=ALU.max, op1=ALU.mult).then_inc(r_done, 1)
                if s.quad(0) is not None:
                    bias(3).then_inc(biased, 1)
                if (n := s.quad(1)) is not None:
                    dve.wait_ge(r_done, n)
                    dve.scalar_tensor_tensor(out=e_sb[:, a], in0=e_sb[:, a], scalar=BIG,
                                             in1=r_inv[:, a].unsqueeze(2).to_broadcast([P, TH, NODES]),
                                             op0=ALU.min, op1=ALU.mult).then_inc(normalised, 1)
                if (p := s.product(1)) is not None:
                    kind, index, par, n = p
                    if kind == "o":
                        if index == 0:
                            dve.wait_ge(x_loaded, s.times(16 * PAIR, 16 * ((s.r - 1) // SPG)))
                        dve.wait_ge(made["o"], n)
                        row = x_sb[:, index, :]
                        dve.tensor_tensor(row, ps_w[1 - b][:, :], row, ALU.add).then_inc(added, 1)
                    else:
                        take_lo(kind, index, n, ps_w[1 - b][:, :], True)
                if (p := s.product(2)) is not None and p[0] == "o":
                    n = p[3]
                    dve.wait_ge(added, n)
                    if not (isinstance(n, int) and n == 1):
                        dve.wait_ge(mean_done, n - 1)
                    dve.bn_stats(ln_stats[:, :], x_sb[:, p[1], :]).then_inc(stats_done, 1)
                if s.i == 2 and (n := s.phase(1)) is not None:
                    f = s.r // GG - 1
                    slot = o_slot(f % TILES, (f // TILES) % PAIR)
                    dve.wait_ge(o_hi_done, n)
                    rest(o_lo[:, slot, :], ps_o[f % 2][:, :], o_hi[:, slot, :]).then_inc(o_lo_done, 1)
                if s.r16 == ADJ_AT and s.group(1) is not None:
                    dve.wait_ge(adj_loaded[1 - s.par], s.times(16, 16 * (s.par + 1)))
                    double_adj(1 - s.par)

            iterations(dve, step)


def kernel(x, adj, L0_gnn_Wq, L0_gnn_Wk, L0_gnn_Wv, L0_gnn_Wo):
    import numpy as np
    import concourse.bacc as bacc
    from concourse.bass_utils import run_bass_kernel_spmd

    x, adj = np.asarray(x), np.asarray(adj)

    def turned(w):
        return np.ascontiguousarray(np.asarray(w).T.reshape(CH, P, D).transpose(1, 0, 2))

    xg = x.reshape(GROUPS, GG, NODES, D)
    arrays = {
        "xt": np.ascontiguousarray(xg.reshape(GROUPS, GG * NODES, CH, P).transpose(0, 2, 3, 1)),
        "x": np.ascontiguousarray(xg.transpose(0, 2, 1, 3)),
        "adj": np.ascontiguousarray(adj.reshape(GROUPS, GG, NODES, NODES).transpose(0, 2, 1, 3)),
        "wq": turned(L0_gnn_Wq),
        "wk": turned(L0_gnn_Wk),
        "wv": turned(L0_gnn_Wv),
        "wo": turned(L0_gnn_Wo),
    }
    nc = bacc.Bacc("TRN2", target_bir_lowering=False, num_devices=1)
    aps = [nc.dram_tensor(name, a.shape, F32, kind="ExternalInput").ap() for name, a in arrays.items()]
    out = nc.dram_tensor("out", [GROUPS, NODES, GG, D], F32, kind="ExternalOutput").ap()
    build(nc, *aps, out)
    r = run_bass_kernel_spmd(nc, [arrays], core_ids=[0])
    got = r.results[0]["out"]
    return np.ascontiguousarray(got.transpose(0, 2, 1, 3)).reshape(GRAPHS, NODES, D)
```
